# Optimizing a Trainium2 kernel written in Bass

```python
import numpy as np
import jax
import jax.numpy as jnp

def _softmax(x, axis=-1):
    return jax.nn.softmax(x, axis=axis)

def _gelu(x):
    return jax.nn.gelu(x, approximate=True)

def _silu(x):
    return jax.nn.silu(x)

def _sigmoid(x):
    return jax.nn.sigmoid(x)

def _layernorm(x, axis=-1, eps=1e-05):
    m = jnp.mean(x, axis=axis, keepdims=True)
    v = jnp.var(x, axis=axis, keepdims=True)
    return (x - m) / jnp.sqrt(v + eps)

def _scatter_add(tgt, idx, src, axis=0):
    return tgt.at[idx].add(src)

def _segment_sum(src, seg, n):
    return jax.ops.segment_sum(src, seg, n)
kernel_name = 'mk_adaln_d1_jaxref_r8_b8d599'

def setup_inputs(seed: int=0):
    np.random.seed(seed)
    _w = jnp.asarray

    def _L0_attn_setup():
        import jax, jax.numpy as jnp
        import numpy as np
        B, T, D, NH = (4, 256, 128, 16)
        HD = D // NH

        def _rwkv7_forward(x, Wr, Wk, Wv, Ww, Wo):
            b, t, d = x.shape
            nh, hd = (NH, d // NH)
            r = jax.nn.sigmoid(x @ Wr.T).reshape(b, t, nh, hd)
            k = (x @ Wk.T).reshape(b, t, nh, hd)
            v = (x @ Wv.T).reshape(b, t, nh, hd)
            w = (jax.nn.sigmoid(x @ Ww.T) * 0.99).reshape(b, t, nh, hd)

            def step(state, inp):
                w_t, k_t, v_t, r_t = inp
                state = state * w_t[..., :, None] + v_t[..., :, None] * k_t[..., None, :]
                out_t = r_t * state.sum(-1)
                return (state, out_t)
            seq = (jnp.moveaxis(w, 1, 0), jnp.moveaxis(k, 1, 0), jnp.moveaxis(v, 1, 0), jnp.moveaxis(r, 1, 0))
            state0 = jnp.zeros((b, nh, hd, hd), dtype=x.dtype)
            _, outs = jax.lax.scan(step, state0, seq)
            out = jnp.moveaxis(outs, 0, 1).reshape(b, t, d)
            eps = jnp.asarray(jnp.finfo(out.dtype).eps, out.dtype)
            out = out * jax.lax.rsqrt(jnp.mean(out * out, axis=-1, keepdims=True) + eps)
            return out @ Wo.T
        key = jax.random.key(seed)
        ks = jax.random.split(key, 6)
        scale = 0.02
        x = jax.random.normal(ks[0], (B, T, D), dtype=jnp.float32)
        Wr = jax.random.normal(ks[1], (D, D), dtype=jnp.float32) * scale
        Wk = jax.random.normal(ks[2], (D, D), dtype=jnp.float32) * scale
        Wv = jax.random.normal(ks[3], (D, D), dtype=jnp.float32) * scale
        Ww = jax.random.normal(ks[4], (D, D), dtype=jnp.float32) * scale
        Wo = jax.random.normal(ks[5], (D, D), dtype=jnp.float32) * scale
        return {'x': x, 'Wr': Wr, 'Wk': Wk, 'Wv': Wv, 'Ww': Ww, 'Wo': Wo}
    _L0_attn_in = _L0_attn_setup()

    def _L0_ffn_setup():
        import jax, jax.numpy as jnp
        import numpy as np
        B, S, H = (2, 256, 128)
        E_ROUTED = 8
        TOP_K = 2
        I = 256
        key = jax.random.key(seed)
        ks = jax.random.split(key, 9)
        s = 0.02
        return {'x': jax.random.normal(ks[0], (B, S, H), dtype=jnp.float32), 'shared_gate': jax.random.normal(ks[1], (I, H), dtype=jnp.float32) * s, 'shared_up': jax.random.normal(ks[2], (I, H), dtype=jnp.float32) * s, 'shared_down': jax.random.normal(ks[3], (H, I), dtype=jnp.float32) * s, 'gate_w': jax.random.normal(ks[4], (E_ROUTED, H, I), dtype=jnp.float32) * s, 'up_w': jax.random.normal(ks[5], (E_ROUTED, H, I), dtype=jnp.float32) * s, 'down_w': jax.random.normal(ks[6], (E_ROUTED, I, H), dtype=jnp.float32) * s, 'router_w': jax.random.normal(ks[7], (E_ROUTED, H), dtype=jnp.float32) * s, 'routing_bias': jnp.zeros((E_ROUTED,), dtype=jnp.float32)}
    _L0_ffn_in = _L0_ffn_setup()
    _L0_c = _w((lambda *s: np.random.randn(*s).astype(np.float32) * 0.05)(8, 128))
    _L0_wmod = _w((lambda *s: np.random.randn(*s).astype(np.float32) * 0.05)(128, 6 * 128) * 128 ** (-0.5))
    _d = {'L0_attn_x': _L0_attn_in['x'], 'L0_attn_Wr': _L0_attn_in['Wr'], 'L0_attn_Wk': _L0_attn_in['Wk'], 'L0_attn_Wv': _L0_attn_in['Wv'], 'L0_attn_Ww': _L0_attn_in['Ww'], 'L0_attn_Wo': _L0_attn_in['Wo'], 'L0_ffn_shared_gate': _L0_ffn_in['shared_gate'], 'L0_ffn_shared_up': _L0_ffn_in['shared_up'], 'L0_ffn_shared_down': _L0_ffn_in['shared_down'], 'L0_ffn_gate_w': _L0_ffn_in['gate_w'], 'L0_ffn_up_w': _L0_ffn_in['up_w'], 'L0_ffn_down_w': _L0_ffn_in['down_w'], 'L0_ffn_router_w': _L0_ffn_in['router_w'], 'L0_ffn_routing_bias': _L0_ffn_in['routing_bias'], 'L0_c': _L0_c, 'L0_wmod': _L0_wmod}
    _x0 = _d['L0_attn_x']
    _d['L0_attn_x'] = jax.random.normal(jax.random.fold_in(jax.random.key(seed), 1), (8, 1024, 128), dtype=_x0.dtype)
    del _x0
    return _d

def reference(L0_attn_x, L0_attn_Wr, L0_attn_Wk, L0_attn_Wv, L0_attn_Ww, L0_attn_Wo, L0_ffn_shared_gate, L0_ffn_shared_up, L0_ffn_shared_down, L0_ffn_gate_w, L0_ffn_up_w, L0_ffn_down_w, L0_ffn_router_w, L0_ffn_routing_bias, L0_c, L0_wmod):

    def _L0_attn_ref(x, Wr, Wk, Wv, Ww, Wo):
        import jax, jax.numpy as jnp
        import numpy as np
        B, T, D, NH = (4, 256, 128, 16)
        HD = D // NH

        def _rwkv7_forward(x, Wr, Wk, Wv, Ww, Wo):
            b, t, d = x.shape
            nh, hd = (NH, d // NH)
            r = jax.nn.sigmoid(x @ Wr.T).reshape(b, t, nh, hd)
            k = (x @ Wk.T).reshape(b, t, nh, hd)
            v = (x @ Wv.T).reshape(b, t, nh, hd)
            w = (jax.nn.sigmoid(x @ Ww.T) * 0.99).reshape(b, t, nh, hd)

            def step(state, inp):
                w_t, k_t, v_t, r_t = inp
                state = state * w_t[..., :, None] + v_t[..., :, None] * k_t[..., None, :]
                out_t = r_t * state.sum(-1)
                return (state, out_t)
            seq = (jnp.moveaxis(w, 1, 0), jnp.moveaxis(k, 1, 0), jnp.moveaxis(v, 1, 0), jnp.moveaxis(r, 1, 0))
            state0 = jnp.zeros((b, nh, hd, hd), dtype=x.dtype)
            _, outs = jax.lax.scan(step, state0, seq)
            out = jnp.moveaxis(outs, 0, 1).reshape(b, t, d)
            eps = jnp.asarray(jnp.finfo(out.dtype).eps, out.dtype)
            out = out * jax.lax.rsqrt(jnp.mean(out * out, axis=-1, keepdims=True) + eps)
            return out @ Wo.T
        return _rwkv7_forward(x, Wr, Wk, Wv, Ww, Wo)

    def _L0_ffn_ref(x, shared_gate, shared_up, shared_down, gate_w, up_w, down_w, router_w, routing_bias):
        import jax, jax.numpy as jnp
        import numpy as np
        B, S, H = (2, 256, 128)
        E_ROUTED = 8
        TOP_K = 2
        I = 256
        b, s, h = x.shape
        shared = jnp.einsum('bsi,hi->bsh', jax.nn.silu(jnp.einsum('bsh,ih->bsi', x, shared_gate)) * jnp.einsum('bsh,ih->bsi', x, shared_up), shared_down)
        logits = jnp.einsum('bsh,eh->bse', x, router_w) + routing_bias
        probs = jax.nn.sigmoid(logits)
        scores, indices = jax.lax.top_k(probs, TOP_K)
        scores = scores / jnp.sum(scores, axis=-1, keepdims=True)
        t = b * s
        xf = x.reshape(t, h)
        idx = indices.reshape(t, TOP_K)
        sc = scores.reshape(t, TOP_K)
        w = jnp.zeros((t, E_ROUTED), dtype=x.dtype)
        w = w.at[jnp.arange(t)[:, None], idx].add(sc)
        g = jax.nn.silu(jnp.einsum('th,ehi->tei', xf, gate_w))
        u = jnp.einsum('th,ehi->tei', xf, up_w)
        combined = jnp.einsum('tei,eih,te->th', g * u, down_w, w)
        return shared + combined.reshape(b, s, h)
    x = L0_attn_x
    mod = (_silu(L0_c) @ L0_wmod).reshape(L0_c.shape[0], 6, 1, -1)
    sa, ca, ga, sb, cb, gb = (mod[:, 0], mod[:, 1], mod[:, 2], mod[:, 3], mod[:, 4], mod[:, 5])
    ga = (2 * (ga >= 0) - 1) * jnp.maximum(jnp.abs(ga), 0.25)
    gb = (2 * (gb >= 0) - 1) * jnp.maximum(jnp.abs(gb), 0.25)
    h = _layernorm(x, axis=-1) * (1 + ca) + sa
    x = x + ga * _L0_attn_ref(h, L0_attn_Wr, L0_attn_Wk, L0_attn_Wv, L0_attn_Ww, L0_attn_Wo)
    h = _layernorm(x, axis=-1) * (1 + cb) + sb
    x = x + gb * _L0_ffn_ref(h, L0_ffn_shared_gate, L0_ffn_shared_up, L0_ffn_shared_down, L0_ffn_gate_w, L0_ffn_up_w, L0_ffn_down_w, L0_ffn_router_w, L0_ffn_routing_bias)
    return x

_drawn_inputs = setup_inputs


def setup_inputs(seed=0):
    import zlib

    import numpy as np

    out = dict(_drawn_inputs(seed))
    spreads = {'L0_ffn_routing_bias': (0.0, 0.8)}
    factors = {'L0_attn_Wr': 8.0,
     'L0_attn_Ww': 8.0,
     'L0_ffn_shared_gate': 8.0,
     'L0_ffn_shared_up': 8.0,
     'L0_ffn_shared_down': 8.0,
     'L0_ffn_gate_w': 8.0,
     'L0_ffn_up_w': 8.0,
     'L0_ffn_down_w': 8.0,
     'L0_ffn_router_w': 8.0}
    for name, (base, spread) in spreads.items():
        noise = np.random.default_rng([zlib.crc32(name.encode()), seed]).standard_normal(out[name].shape)
        drawn = base * np.exp(spread * noise) if base else spread * noise
        out[name] = jnp.asarray(drawn.astype(out[name].dtype))
    for name, factor in factors.items():
        out[name] = (out[name] * factor).astype(out[name].dtype)
    return out
```

```python
from contextlib import ExitStack

import concourse.bass as bass
from concourse import mybir

ALU = mybir.AluOpType
ACT = mybir.ActivationFunctionType
F32 = mybir.dt.float32
BF16 = mybir.dt.bfloat16
I32 = mybir.dt.int32
U32 = mybir.dt.uint32
AX_X = mybir.AxisListType.X

P = 128


def need(engine, semaphore, count):
    if isinstance(count, int) and count <= 0:
        return
    engine.wait_ge(semaphore, count)


def wait_apart(engine, semaphore, count, met):
    if not isinstance(count, int):
        count = engine.to_reg(count)
    engine.wait_ge(met, 1)
    engine.wait_ge(semaphore, count)


def landed(k, slot, ring, each=16):
    return (each // ring) * k + (each - (each // ring) * slot)


def build(nc, x, Wr, Wk, Wv, Ww, Wo, shared_gate, shared_up, shared_down, gate_w, up_w, down_w,
          router_w, routing_bias, c, wmod, out):
    NB, T, D = x.shape
    NH = 16
    HD = D // NH
    E, _, I = gate_w.shape
    M = I // P
    K = 2
    NT = T // P
    CH = 512
    NC = T // CH
    TC = CH // P
    TOKENS = NB * T
    CAP = TOKENS
    BODY = 4
    TILES = -(-(TOKENS * K // P + E - 1) // BODY) * BODY
    SPARE_TILES = TILES - TOKENS * K // P
    SPARE0 = E * CAP
    TRASH0 = SPARE0 + SPARE_TILES * P
    ROWS = TRASH0 + E * P
    W = 132
    YPAD0 = TOKENS * K
    YROWS = YPAD0 + E * P + SPARE_TILES * P
    LN_EPS = 1e-5
    RMS_EPS = 1.1920928955078125e-07

    with ExitStack() as ctx:
        def sb(name, shape, dt=F32):
            return ctx.enter_context(nc.sbuf_tensor(name, shape, dt))

        def sem(name):
            return ctx.enter_context(nc.semaphore(name))

        bank = [ctx.enter_context(nc.psum_tensor(f"bank{i}", [P, 512], F32)) for i in range(8)]

        expert_rows = nc.dram_tensor("expert_rows", (ROWS, W), F32).ap()
        result_rows = nc.dram_tensor("result_rows", (YROWS, D), F32).ap()
        mod_rows = nc.dram_tensor("mod_rows", (NB, 4 * D), F32).ap()

        ident = sb("ident", [P, P])
        head_ones = sb("head_ones", [P, P])
        before = sb("before", [P, P], BF16)
        ones_bf = sb("ones_bf", [P, P], BF16)
        ones_col = sb("ones_col", [P, 2])
        minus_half = sb("minus_half", [P, NT])
        tile_start = sb("tile_start", [P, E * NT])
        iota_i = sb("iota_i", [P, 256], I32)
        expert_iota = sb("expert_iota", [P, E])
        region_rows = sb("region_rows", [P, E])
        running = sb("running", [P, E])
        dest_next = sb("dest_next", [P, NT, K])
        lane = sb("lane", [P, 1])
        pad_dest = sb("pad_dest", [P, E])
        trash_row = sb("trash_row", [P, E])

        rraw = sb("rraw", [E, P])
        craw = sb("craw", [NB, D])
        bias_row = sb("bias_row", [P, E])
        WrT = sb("WrT", [P, P])
        WvT = sb("WvT", [P, P])
        WwT = sb("WwT", [P, P])
        WksT = sb("WksT", [P, P])
        WoT = sb("WoT", [P, P])
        Wo_b = sb("Wo_b", [P, P])
        SgT = sb("SgT", [P, I])
        SuT = sb("SuT", [P, I])
        SdT = sb("SdT", [P, M, P])
        Sd_b = sb("Sd_b", [P, M, P])
        RwT = sb("RwT", [P, E])
        WE = 2 * I + M * D
        Wexp = sb("Wexp", [P, E * WE])

        csilu = sb("csilu", [NB, D])
        csiluT = sb("csiluT", [P, NB])
        mod_sb = sb("mod_sb", [NB, 6, D])
        sign_sb = sb("sign_sb", [NB, 2, D])
        mag_sb = sb("mag_sb", [NB, 2, D])
        mod_col = sb("mod_col", [P, NB * 2])
        cur_col = sb("cur_col", [P, 2])
        mod_row = sb("mod_row", [P, NB * 4 * D])

        xb = [sb(f"xb{i}", [P, NT, D]) for i in range(2)]
        stats1 = sb("stats1", [P, NT, 6])
        mv1 = sb("mv1", [P, NT, 2])
        var1 = sb("var1", [P, NT])
        rstd1 = sb("rstd1", [P, NT])
        xn1 = sb("xn1", [P, NT, D])
        h1T = sb("h1T", [P, T])
        rT = sb("rT", [P, T])
        wsig = sb("wsig", [P, T])
        ksT = sb("ksT", [P, T])
        stateT = sb("stateT", [P, T])
        outT = sb("outT", [P, T])
        sqT = sb("sqT", [P, T])
        wraw = sqT[:, 0:5 * P].rearrange("p (i n) -> p i n", i=5)
        sgraw = outT[:, 0:I].rearrange("p (m n) -> p m n", m=M)
        suraw = outT[:, I:2 * I].rearrange("p (m n) -> p m n", m=M)
        sdraw = outT[:, 2 * I:3 * I]
        wmod_sb = stateT[:, 0:6 * D]
        resid = sb("resid", [P, NB * NT * D])
        var3 = sb("var3", [P, NT])
        rstd3 = sb("rstd3", [P, NT])
        stats2 = sb("stats2", [P, NT, 6])
        mv2 = sb("mv2", [P, NT, 2])
        var2 = sb("var2", [P, NT])
        rstd2 = sb("rstd2", [P, NT])
        xn2 = sb("xn2", [P, NT, D])
        rows = [sb(f"rows{i}", [P, NT, K, W]) for i in range(2)]
        h2T = [sb(f"h2T{i}", [P, T]) for i in range(2)]
        logits = sb("logits", [P, NT, E])
        probs = sb("probs", [P, NT, E])
        top = sb("top", [P, NT, 8])
        topi = sb("topi", [P, NT, 8], U32)
        topf = sb("topf", [P, K, NT])
        onehot = sb("onehot", [P, K, NT, E])
        picks = sb("picks", [P, E * NT], BF16)
        picks_sum = sb("picks_sum", [P, E * NT], BF16)
        picks_before = sb("picks_before", [P, E * NT], BF16)
        den = sb("den", [P, NT])
        rden = sb("rden", [P, NT])
        pos = sb("pos", [P, E * NT])
        prod = sb("prod", [P, K, NT, E])
        slotf = sb("slotf", [P, K * NT])
        slots = sb("slots", [P, K * NT], I32)
        sg = sb("sg", [P, 4, CH])
        guT = sb("guT", [P, M, T])
        counts = sb("counts", [P, E])
        tmpf = sb("tmpf", [P, E])
        tmpi = sb("tmpi", [P, E], I32)
        tilesi = sb("tilesi", [P, E], I32)
        tilesf = sb("tilesf", [P, E])
        modi = sb("modi", [P, E], I32)
        modf = sb("modf", [P, E])
        ends = sb("ends", [P, E])
        skip = sb("skip", [P, E])
        ones_e = sb("ones_e", [P, E])
        padr = sb("padr", [P, E])
        padv = sb("padv", [P, E])
        padd = sb("padd", [P, E])
        pad_slot = sb("pad_slot", [P, E], I32)
        pad_rows = sb("pad_rows", [P, E, W])
        spare_rows = sb("spare_rows", [P, SPARE_TILES, W])
        tile_iota = sb("tile_iota", [1, TILES])
        passed = guT[0:1].rearrange("a m n -> a (m n)")[:, 0:TILES * E].rearrange("a (j e) -> a j e", e=E)
        passed_skip = sg[0:1].rearrange("a m n -> a (m n)")[:, 0:TILES * E].rearrange("a (j e) -> a j e", e=E)
        tab_f = sb("tab_f", [1, 2, TILES])
        tab_g = sb("tab_g", [1, 2, TILES])
        tab = sb("tab", [1, 2 * TILES], I32)
        XR = 4
        xt = [sb(f"xt{i}", [P, W]) for i in range(XR)]
        meta = [sb(f"meta{i}", [P, 2]) for i in range(XR)]
        xT = [sb(f"xT{i}", [P, P]) for i in range(2)]
        sge = [sb(f"sge{i}", [P, I]) for i in range(2)]
        pe_in = [sb(f"gu{i}", [P, I]) for i in range(2)]
        guTe = [sb(f"guTe{i}", [P, I]) for i in range(2)]
        ye = [sb(f"ye{i}", [P, D]) for i in range(XR)]
        yb = [rows[i][:].rearrange("p t k w -> p (t k w)")[:, 0:CH * K].rearrange("p (t k d) -> p t k d", k=K, d=D)
              for i in range(2)]
        acc = [h1T[:, i * CH:(i + 1) * CH].rearrange("p (t d) -> p t d", d=D) for i in range(2)]
        fin = [rT[:, i * CH:(i + 1) * CH].rearrange("p (t d) -> p t d", d=D) for i in range(2)]

        S = {}
        for name in (
            "attn_w_loaded", "mod_w_loaded", "ffn_w_loaded", "expert_w_loaded", "mod_stored", "mod_row_loaded",
            "pool_const", "ident_ready", "iota_done", "dve_const", "setup_psum", "setup_copied", "csilu_ready", "mod_step",
            "mod_ready",
            "stats1_done", "mv1_done", "var1_ready", "rstd1_ready", "col_ready", "xn1_ready",
            "xT_ready", "h1T_ready", "r_ready", "w_ready", "ks_ready", "v_ready", "r_done", "w_done", "ks_done",
            "decay_done", "kv_done", "state_done", "out_ready", "sq_ready",
            "ss_ready", "var3_ready", "rstd3_ready", "wo_scaled", "wo_ready", "x1_ready", "stats2_done", "mv2_done",
            "var2_ready", "rstd2_ready", "xn2_done", "h2_scaled", "h2_ready", "h2xT_ready", "h2T_ready",
            "rows2_ready", "logits_psum", "logits_ready", "probs_ready", "top_done", "topi_done", "topf_done", "onehot_done",
            "picks_done", "picks_sum_done", "picks_ready", "den_done", "rden_done", "meta_ready",
            "pos_ready", "pos_done", "prod_done", "slotf_done", "slots_ready", 
            "gate_ready", "up_ready", "silu_ready", "gu_ready", "sd_scaled", "down_ready", "base_ready",
            "table_step", "table_ready", "spare_ready", "spare_stored", "pad_ready", "pads_scattered",
            "xtT_ready", "xT_done", "gate_up_ready", "silu_done", "meta_done", "gu_done", "guT_psum", "guT_done",
            "y_psum", "y_done", 
            "y_sum", "y_gated", "fin_ready", 
        ):
            S[name] = sem(name)
        x_loaded = [sem(f"x_loaded{i}") for i in range(2)]
        rows_scattered = [sem(f"rows_scattered{i}") for i in range(2)]
        xt_loaded = [sem(f"xt_loaded{i}") for i in range(XR)]
        y_scattered = [sem(f"y_scattered{i}") for i in range(XR)]
        yb_loaded = [sem(f"yb_loaded{i}") for i in range(2)]
        out_stored = [sem(f"out_stored{i}") for i in range(2)]

        x_v = x.rearrange("b (t p) d -> p (b t) d", p=P)
        res_v = resid[:, :]
        out_v = out.rearrange("b (t p) d -> p (b t) d", p=P)
        y_v = result_rows[0:TOKENS * K, :].rearrange("(n p k) d -> p n k d", p=P, k=K)

        def mod_at(b, which):
            return mod_row[:, bass.ds((b * 4 + which) * D, D)]

        def resid_tiles(b, t, n):
            return res_v[:, bass.ds((b * NT + t) * D, n * D)]

        b_T, b_small = bank[0], bank[1]
        b_proj = [bank[2], bank[3]]
        b_O = [bank[4], bank[5]]
        b_gate = [bank[6], bank[2]]
        b_up = [bank[7], bank[3]]
        SS, LG, PO, CN = 0, 8, 8 + NT * E, 8 + 2 * NT * E

        block = ctx.enter_context(nc.Block())

        def pipeline(eng, step):
            step(-1, 1, True, False, False)
            step(0, 0, True, True, False)
            step(1, 1, True, True, True)
            with eng.Fori(2, NB - 3, 2) as b:
                step(b, 0, True, True, True)
                step(b + 1, 1, True, True, True)
            step(NB - 2, 0, True, True, True)
            step(NB - 1, 1, False, True, True)
            step(NB, 0, False, False, True)

        @block.sync
        def _(sp):
            sp.dma_start(craw[:], c).then_inc(S["mod_w_loaded"], 16)
            sp.dma_start(wmod_sb, wmod).then_inc(S["mod_w_loaded"], 16)
            for i, w in enumerate((Wr, Wk, Wv, Ww, Wo)):
                sp.dma_start(wraw[:, i, :], w).then_inc(S["attn_w_loaded"], 16)
            for b in range(2):
                sp.dma_start(xb[b][:], x_v[:, b * NT:(b + 1) * NT, :]).then_inc(x_loaded[b], 16)
            sp.dma_start(sgraw, shared_gate.rearrange("(m p) h -> p m h", p=P)).then_inc(S["ffn_w_loaded"], 16)
            sp.dma_start(suraw, shared_up.rearrange("(m p) h -> p m h", p=P)).then_inc(S["ffn_w_loaded"], 16)
            sp.dma_start(sdraw, shared_down).then_inc(S["ffn_w_loaded"], 16)
            sp.dma_start(rraw[:], router_w).then_inc(S["ffn_w_loaded"], 16)
            sp.dma_start(bias_row[:], routing_bias.rearrange("(a e) -> a e", a=1).to_broadcast([P, E]))\
                .then_inc(S["ffn_w_loaded"], 16)
            sp.wait_ge(S["mod_ready"], 1)
            sp.dma_start(mod_rows, mod_sb[:, 2:6, :].rearrange("b m d -> b (m d)")).then_inc(S["mod_stored"], 16)
            sp.wait_ge(S["mod_stored"], 16)
            sp.dma_start(mod_row[:], mod_rows.rearrange("b n -> (b n)").rearrange("(a n) -> a n", a=1)
                         .to_broadcast([P, NB * 4 * D])).then_inc(S["mod_row_loaded"], 16)
            for e in range(E):
                wg = Wexp[:, e * WE:(e + 1) * WE]
                sp.dma_start(wg[:, 0:I], gate_w[e]).then_inc(S["expert_w_loaded"], 16)
                sp.dma_start(wg[:, I:2 * I], up_w[e]).then_inc(S["expert_w_loaded"], 16)
                sp.dma_start(wg[:, 2 * I:WE].rearrange("p (m h) -> p m h", m=M),
                             down_w[e].rearrange("(m p) h -> p m h", p=P)).then_inc(S["expert_w_loaded"], 16)
            sp.wait_ge(S["spare_ready"], 1)
            sp.dma_start(expert_rows[SPARE0:TRASH0, :].rearrange("(n p) w -> p n w", p=P), spare_rows[:])\
                .then_inc(S["spare_stored"], 16)

            def load_x(b, par):
                sp.wait_ge(S["x1_ready"], b - 1)
                sp.dma_start(xb[par][:], x_v[:, bass.ds(b * NT, NT), :]).then_inc(x_loaded[par], 16)

            with sp.Fori(2, NB - 1, 2) as b:
                load_x(b, 0)
                load_x(b + 1, 1)

            def load_tile(j, r):
                first = sp.value_load(tab[0:1, bass.ds(TILES + j, 1)], min_val=0, max_val=SPARE0 + (SPARE_TILES - 1) * P)
                need(sp, S["xtT_ready"], j - XR + 1)
                need(sp, S["meta_done"], j - XR + 1)
                sp.dma_start(xt[r][:], expert_rows[bass.ds(first, P), :]).then_inc(xt_loaded[r], 16)

            sp.wait_ge(S["table_ready"], 1)
            for i in range(2):
                sp.wait_ge(rows_scattered[i], 16 * NT * K * NB // 2)
            sp.wait_ge(S["pads_scattered"], 16 * E)
            sp.wait_ge(S["spare_stored"], 16)
            for j in range(XR):
                load_tile(j, j)
            with sp.Fori(XR, TILES - XR + 1, XR) as j:
                for r in range(XR):
                    load_tile(j + r, r)

            def load_y(n, r):
                need(sp, S["y_sum"], n - 1)
                sp.dma_start(yb[r], y_v[:, bass.ds(n * TC, TC), :, :]).then_inc(yb_loaded[r], 16)

            def store(n, r):
                sp.wait_ge(S["fin_ready"], n + 1)
                sp.dma_start(out_v[:, bass.ds(n * TC, TC), :], fin[r]).then_inc(out_stored[r], 16)

            for r in range(XR):
                sp.wait_ge(y_scattered[r], 16 * TILES // XR)
            load_y(0, 0)
            load_y(1, 1)
            with sp.Fori(0, NB * NC - 3, 2) as n:
                for r in range(2):
                    load_y(n + 2 + r, r)
                    store(n + r, r)
            for n in range(NB * NC - 2, NB * NC):
                store(n, n % 2)
            for r in range(2):
                sp.wait_ge(out_stored[r], 16 * NB * NC // 2)

        @block.gpsimd
        def _(pool):
            pool.memset(ident[:], 0.0).then_inc(S["pool_const"], 1)
            pool.memset(head_ones[:], 1.0).then_inc(S["pool_const"], 1)
            pool.memset(before[:], 1.0).then_inc(S["pool_const"], 1)
            pool.memset(ones_bf[:], 1.0).then_inc(S["pool_const"], 1)
            pool.memset(ones_col[:], 1.0).then_inc(S["pool_const"], 1)
            pool.memset(minus_half[:], -0.5).then_inc(S["pool_const"], 1)
            pool.memset(pad_rows[:], 0.0).then_inc(S["pool_const"], 1)
            pool.memset(spare_rows[:], 0.0).then_inc(S["pool_const"], 1)
            for i in range(2):
                pool.memset(rows[i][:, :, :, D:W], 0.0).then_inc(S["pool_const"], 1)
            pool.memset(tile_start[:], 1.0).then_inc(S["pool_const"], 1)
            pool.memset(ones_e[:], 1.0).then_inc(S["pool_const"], 1)
            pool.wait_ge(S["pool_const"], 12)
            pool.affine_select(out=ident[:], in_=ident[:], compare_op=ALU.not_equal, fill=1.0, base=0,
                               pattern=[[-1, P]], channel_multiplier=1).then_inc(S["ident_ready"], 1)
            hv = head_ones[:].rearrange("p (g r) -> p g r", r=HD)
            pool.affine_select(out=hv, in_=hv, compare_op=ALU.is_ge, fill=0.0, base=0,
                               pattern=[[-HD, NH], [0, HD]], channel_multiplier=1).then_inc(S["ident_ready"], 1)
            pool.affine_select(out=before[:], in_=before[:], compare_op=ALU.is_gt, fill=0.0, base=0,
                               pattern=[[1, P]], channel_multiplier=-1).then_inc(S["ident_ready"], 1)
            tv = tile_start[:].rearrange("p (e t) -> p e t", e=E)
            pool.affine_select(out=tv, in_=tv, compare_op=ALU.not_equal, fill=0.0, base=0,
                               pattern=[[0, E], [1, NT]], channel_multiplier=0).then_inc(S["ident_ready"], 1)
            pool.wait_ge(S["ident_ready"], 4)
            pool.affine_select(out=hv, in_=hv, compare_op=ALU.is_ge, fill=0.0, base=HD - 1,
                               pattern=[[HD, NH], [0, HD]], channel_multiplier=-1).then_inc(S["ident_ready"], 1)
            iotas = [
                (iota_i[:, 0:E], [[1, E]], 0, 0),
                (iota_i[:, E:2 * E], [[CAP, E]], 0, 0),
                (iota_i[:, 2 * E:2 * E + NT * K], [[K * P, NT], [1, K]], 0, K),
                (iota_i[:, 32:33], [[1, 1]], 0, 1),
                (iota_i[:, 40:40 + E], [[P, E]], YPAD0, 1),
                (iota_i[:, 48:48 + E], [[P, E]], TRASH0, 1),
                (iota_i[:, 56:56 + SPARE_TILES], [[P, SPARE_TILES]], YPAD0 + E * P, 1),
                (iota_i[0:1, 64:64 + TILES], [[1, TILES]], 0, 0),
            ]
            for o, pattern, base, cm in iotas:
                pool.iota(o, pattern=pattern, base=base, channel_multiplier=cm).then_inc(S["iota_done"], 1)

            def power(out_, in_, ready, b, done):
                pool.wait_ge(ready, b + 1)
                pool.tensor_tensor(out_[:], in_[:], minus_half[:], ALU.pow).then_inc(done, 1)

            def scatter(b, par, columns):
                for q in columns:
                    pool.indirect_dma_start(
                        expert_rows, bass.IndirectOffsetOnAxis(ap=slots[:, q:q + 1], axis=0),
                        rows[par][:, q % NT, q // NT, :], None).then_inc(rows_scattered[par], 16)

            def step(b, par, front, middle, back):
                if front:
                    power(rstd1, var1, S["var1_ready"], b + 1, S["rstd1_ready"])
                if middle:
                    power(rstd3, var3, S["var3_ready"], b, S["rstd3_ready"])
                if back:
                    wait_apart(pool, S["slots_ready"], b, S["pool_const"])
                    pool.wait_ge(S["rows2_ready"], b)
                    pool.wait_ge(S["meta_ready"], b)
                    scatter(b - 1, 1 - par, range(0, 4))
                if middle:
                    power(rstd2, var2, S["var2_ready"], b, S["rstd2_ready"])
                if back:
                    scatter(b - 1, 1 - par, range(4, NT * K))

            pipeline(pool, step)

            pool.wait_ge(S["pad_ready"], 1)
            for e in range(E):
                pool.indirect_dma_start(
                    expert_rows, bass.IndirectOffsetOnAxis(ap=pad_slot[:, e:e + 1], axis=0),
                    pad_rows[:, e, :], None).then_inc(S["pads_scattered"], 16)

            def put(j, r):
                wait_apart(pool, S["y_done"], j + 1, S["pool_const"])
                pool.indirect_dma_start(
                    result_rows, bass.IndirectOffsetOnAxis(ap=meta[r][:, 0:1].bitcast(I32), axis=0),
                    ye[r][:], None).then_inc(y_scattered[r], 16)

            with pool.Fori(0, TILES - BODY + 1, BODY) as j:
                for r in range(BODY):
                    put(j + r, r)

        @block.tensor
        def _(pe):
            pe.wait_ge(S["ident_ready"], 5)
            pe.wait_ge(S["attn_w_loaded"], 16 * 5)
            pe.transpose(bank[0][:, 0:P], wraw[:, 0, :], ident[:])
            pe.transpose(bank[0][:, P:2 * P], wraw[:, 2, :], ident[:])
            pe.transpose(bank[0][:, 2 * P:3 * P], wraw[:, 3, :], ident[:])
            pe.transpose(bank[0][:, 3 * P:4 * P], wraw[:, 4, :], ident[:])
            pe.matmul(bank[1][:, 0:P], wraw[:, 1, :], head_ones[:], start=True, stop=True)\
                .then_inc(S["setup_psum"], 1)
            pe.wait_ge(S["mod_w_loaded"], 32)
            pe.wait_ge(S["csilu_ready"], 1)
            pe.transpose(bank[2][:, 0:NB], csilu[:], ident[0:NB, 0:NB]).then_inc(S["setup_psum"], 1)
            pe.wait_ge(S["setup_copied"], 2)
            half = 3 * D
            pe.matmul(bank[3][0:NB, 0:half], csiluT[:], wmod_sb[:, 0:half], start=True, stop=True)
            pe.matmul(bank[4][0:NB, 0:half], csiluT[:], wmod_sb[:, half:2 * half], start=True, stop=True)
            pe.matmul(bank[5][:, 0:NB], wmod_sb[:, 0:D], csiluT[:], start=True, stop=True)
            pe.matmul(bank[5][:, NB:2 * NB], wmod_sb[:, D:2 * D], csiluT[:], start=True, stop=True)\
                .then_inc(S["setup_psum"], 1)
            pe.wait_ge(S["ffn_w_loaded"], 16 * 5)
            for m in range(M):
                pe.transpose(bank[6][:, m * P:(m + 1) * P], sgraw[:, m, :], ident[:])
                pe.transpose(bank[6][:, (M + m) * P:(M + m + 1) * P], suraw[:, m, :], ident[:])
                pe.transpose(bank[7][:, m * P:(m + 1) * P], sdraw[:, m * P:(m + 1) * P], ident[:])
            pe.transpose(bank[7][:, M * P:M * P + E], rraw[:], ident[0:E, 0:E]).then_inc(S["setup_psum"], 1)
            pe.wait_ge(S["setup_copied"], 4)

            def step(b, par, front, middle, back):
                f, g, h = b + 1, b, b - 1
                if back:
                    pe.wait_ge(S["picks_ready"], h + 1)
                    pe.matmul(b_small[:, PO:PO + E * NT], before[:], picks[:], start=True, stop=False)
                    pe.matmul(b_small[:, PO:PO + E * NT], ones_bf[:], picks_before[:], start=False, stop=True)
                    pe.matmul(b_small[:, CN:CN + E], ones_bf[:], picks_sum[:, NT - 1:E * NT:NT], start=True, stop=True)\
                        .then_inc(S["pos_ready"], 1)
                if middle:
                    pe.wait_ge(S["sq_ready"], NC * (g + 1))
                    need(pe, S["logits_ready"], g)
                    for t in range(NT):
                        last = pe.matmul(b_small[:, SS + t:SS + t + 1], sqT[:, t * P:(t + 1) * P], ones_col[:, 0:1],
                                         start=True, stop=True)
                    last.then_inc(S["ss_ready"], 1)
                    pe.wait_ge(S["wo_scaled"], g + 1)
                    need(pe, S["base_ready"], NC * (g - 1) if isinstance(g, int) else NC * g - NC)
                    for n in range(NC):
                        for t in range(TC):
                            at = (n * TC + t) * P
                            last = pe.matmul(b_O[n][:, t * P:(t + 1) * P], outT[:, at:at + P], Wo_b[:],
                                             start=True, stop=True)
                        last.then_inc(S["wo_ready"], 1)
                if back:
                    for n in range(NC):
                        for m in range(M):
                            q = n * M + m
                            if q < 2:
                                need(pe, S["gu_ready"], 4 * h)
                                if q == 1:
                                    pe.wait_ge(S["ks_done"], NC * (g + 1) if front or middle else NC * NB)
                                    pe.wait_ge(S["kv_done"], NC * (g + 1) if front or middle else NC * NB)
                            else:
                                pe.wait_ge(S["gu_ready"], 4 * h + q - 1)
                            pe.matmul(b_gate[q % 2][:], SgT[:, m * P:(m + 1) * P], h2T[1 - par][:, n * CH:(n + 1) * CH],
                                      start=True, stop=True).then_inc(S["gate_ready"], 1)
                            pe.matmul(b_up[q % 2][:], SuT[:, m * P:(m + 1) * P], h2T[1 - par][:, n * CH:(n + 1) * CH],
                                      start=True, stop=True).then_inc(S["up_ready"], 1)
                if front:
                    pe.wait_ge(S["xn1_ready"], f + 1)
                    for n in range(NC):
                        if n == 0:
                            need(pe, S["h2T_ready"], NC * (f - 1))
                        else:
                            pe.wait_ge(S["h1T_ready"], NC * f + n)
                        for t in range(TC):
                            last = pe.transpose(b_T[:, t * P:(t + 1) * P], xn1[:, n * TC + t, :], ident[:])
                        last.then_inc(S["xT_ready"], 1)
                    for n in range(NC):
                        at = slice(n * CH, (n + 1) * CH)
                        pe.wait_ge(S["h1T_ready"], NC * f + n + 1)
                        if n == 0:
                            if back:
                                pe.wait_ge(S["gu_ready"], 4 * h + 4)
                            need(pe, S["ks_done"], NC * f)
                            need(pe, S["kv_done"], NC * f)
                        else:
                            pe.wait_ge(S["ks_done"], NC * f + n)
                        pe.matmul(b_proj[0][:], WrT[:], h1T[:, at], start=True, stop=True).then_inc(S["r_ready"], 1)
                        if n > 0:
                            pe.wait_ge(S["kv_done"], NC * f + n)
                        pe.matmul(b_proj[1][:], WwT[:], h1T[:, at], start=True, stop=True).then_inc(S["w_ready"], 1)
                        pe.wait_ge(S["r_done"], NC * f + n + 1)
                        pe.matmul(b_proj[0][:], WksT[:], h1T[:, at], start=True, stop=True).then_inc(S["ks_ready"], 1)
                        pe.wait_ge(S["w_done"], NC * f + n + 1)
                        pe.matmul(b_proj[1][:], WvT[:], h1T[:, at], start=True, stop=True).then_inc(S["v_ready"], 1)
                if back:
                    pe.wait_ge(S["gu_ready"], 4 * h + 4)
                    pe.wait_ge(S["sd_scaled"], h + 1)
                    pe.wait_ge(S["x1_ready"], (g + 1) if middle else NB)
                    for n in range(NC):
                        for t in range(TC):
                            at = (n * TC + t) * P
                            for m in range(M):
                                last = pe.matmul(b_O[n][:, t * P:(t + 1) * P], guT[:, m, at:at + P], Sd_b[:, m, :],
                                                 start=(m == 0), stop=(m == M - 1))
                        last.then_inc(S["down_ready"], 1)
                if middle:
                    pe.wait_ge(S["h2_ready"], g + 1)
                    for n in range(NC):
                        if n == 0:
                            pe.wait_ge(S["h1T_ready"], NC * (g + 2) if front else NC * NB)
                        else:
                            pe.wait_ge(S["h2T_ready"], NC * g + n)
                        for t in range(TC):
                            last = pe.transpose(b_T[:, t * P:(t + 1) * P], rows[par][:, n * TC + t, 0, 0:D], ident[:])
                        last.then_inc(S["h2xT_ready"], 1)
                    pe.wait_ge(S["h2T_ready"], NC * (g + 1))
                    pe.wait_ge(S["var3_ready"], g + 1)
                    need(pe, S["pos_done"], g)
                    for t in range(NT):
                        last = pe.matmul(b_small[:, LG + t * E:LG + (t + 1) * E], h2T[par][:, t * P:(t + 1) * P],
                                         RwT[:], start=True, stop=True)
                    last.then_inc(S["logits_psum"], 1)

            pipeline(pe, step)

            bx = [bank[0], bank[1]]
            bgu = [bank[2], bank[3]]
            bp = [bank[6], bank[7]]
            by = [bank[4], bank[5]]

            def turn(j, r):
                pe.wait_ge(xt_loaded[r], landed(j, r, XR))
                pe.transpose(bx[r % 2][:, 0:P], xt[r][:, 0:P], ident[:]).then_inc(S["xtT_ready"], 1)

            def gate_up(j, r, e):
                pe.wait_ge(S["xT_done"], j + 1)
                pe.matmul(bgu[r % 2][:], xT[r % 2][:], Wexp[:, bass.ds(e, 2 * I)], start=True, stop=True)\
                    .then_inc(S["gate_up_ready"], 1)

            def turn_gu(j, r):
                pe.wait_ge(S["gu_done"], j + 1)
                for m in range(M):
                    if m == M - 1:
                        need(pe, S["y_done"], j - 2)
                    last = pe.transpose(bp[r % 2][:, m * P:(m + 1) * P], pe_in[r % 2][:, m * P:(m + 1) * P], ident[:])
                last.then_inc(S["guT_psum"], 1)

            def down(j, r, e):
                pe.wait_ge(S["guT_done"], j + 1)
                for m in range(M):
                    last = pe.matmul(by[r % 2][:, 0:D], guTe[r % 2][:, m * P:(m + 1) * P],
                                     Wexp[:, bass.ds(e + (2 * I + m * D), D)], start=(m == 0), stop=(m == M - 1))
                last.then_inc(S["y_psum"], 1)

            def experts_of(j, n):
                return list(nc.values_load_multi_w_load_instructions(
                    tab[0:1, bass.ds(j, n)], engines=[mybir.EngineType.PE], min_val=0, max_val=(E - 1) * WE,
                    
                    skip_runtime_bounds_check_because="the table's values are clamped")[1])

            pe.wait_ge(S["base_ready"], NB * NC)
            pe.wait_ge(S["h2T_ready"], NB * NC)
            pe.wait_ge(S["pos_done"], NB)
            pe.wait_ge(S["expert_w_loaded"], 16 * 3 * E)
            pe.wait_ge(S["table_ready"], 1)
            e = experts_of(0, BODY + 2)
            turn(0, 0)
            turn(1, 1)
            gate_up(0, 0, e[0])
            turn(2, 2)
            gate_up(1, 1, e[1])
            turn_gu(0, 0)

            def step_e(j, r, e_prev, e_next, turns=True, gates=True):
                if turns:
                    turn(j + 2, (r + 2) % BODY)
                if gates:
                    gate_up(j + 1, (r + 1) % BODY, e_next)
                turn_gu(j, r)
                down(j - 1, (r - 1) % BODY, e_prev)

            for j in range(1, BODY + 1):
                step_e(j, j % BODY, e[j - 1], e[j + 1])
            with pe.Fori(BODY + 1, TILES - 2 - BODY, BODY) as j:
                e = experts_of(j - 1, BODY)
                ahead = experts_of(j + (BODY - 1), 2)
                e = e + ahead
                for q in range(BODY):
                    step_e(j + q, (1 + q) % BODY, e[q], e[q + 2])
            e = experts_of(TILES - BODY, BODY)
            for j in range(TILES - 3, TILES):
                q = j - (TILES - BODY)
                step_e(j, j % BODY, e[q - 1], e[q + 1] if j + 1 < TILES else None,
                       turns=j + 2 < TILES, gates=j + 1 < TILES)
            down(TILES - 1, (TILES - 1) % BODY, e[BODY - 1])

        @block.scalar
        def _(act):
            act.wait_ge(S["mod_w_loaded"], 32)
            act.activation(csilu[:], craw[:], ACT.Silu).then_inc(S["csilu_ready"], 1)

            def step(b, par, front, middle, back):
                f, g, h = b + 1, b, b - 1
                if back:
                    for q in range(NC * M):
                        act.wait_ge(S["gate_ready"], 4 * h + q + 1)
                        need(act, S["gu_ready"], 4 * h)
                        act.activation(sg[:, q, :], b_gate[q % 2][:], ACT.Silu).then_inc(S["silu_ready"], 1)
                if front:
                    act.wait_ge(S["col_ready"], f + 1)
                    for n in range(NC):
                        act.wait_ge(S["xT_ready"], NC * f + n + 1)
                        need(act, S["v_ready"], NC * f)
                        act.activation(h1T[:, n * CH:(n + 1) * CH], b_T[:], ACT.Identity, bias=cur_col[:, 0:1],
                                       scale=cur_col[:, 1:2]).then_inc(S["h1T_ready"], 1)
                    need(act, S["out_ready"], NC * f)
                    for n in range(NC):
                        at = slice(n * CH, (n + 1) * CH)
                        act.wait_ge(S["r_ready"], NC * f + n + 1)
                        act.activation(rT[:, at], b_proj[0][:], ACT.Sigmoid).then_inc(S["r_done"], 1)
                        act.wait_ge(S["w_ready"], NC * f + n + 1)
                        act.activation(wsig[:, at], b_proj[1][:], ACT.Sigmoid).then_inc(S["w_done"], 1)
                        act.wait_ge(S["ks_ready"], NC * f + n + 1)
                        act.activation(ksT[:, at], b_proj[0][:], ACT.Copy).then_inc(S["ks_done"], 1)
                    for n in range(NC):
                        at = slice(n * CH, (n + 1) * CH)
                        act.wait_ge(S["out_ready"], NC * f + n + 1)
                        need(act, S["ss_ready"], f)
                        act.activation(sqT[:, at], outT[:, at], ACT.Square).then_inc(S["sq_ready"], 1)
                if middle:
                    act.wait_ge(S["h2_ready"], g + 1)
                    act.activation(rows[par][:, :, 1, 0:D], rows[par][:, :, 0, 0:D], ACT.Copy).then_inc(S["rows2_ready"], 1)
                    need(act, S["up_ready"], 4 * (g - 1) if isinstance(g, int) else 4 * g - 4)
                    for n in range(NC):
                        act.wait_ge(S["h2xT_ready"], NC * g + n + 1)
                        act.activation(h2T[par][:, n * CH:(n + 1) * CH], b_T[:], ACT.Copy).then_inc(S["h2T_ready"], 1)
                    act.wait_ge(S["logits_ready"], g + 1)
                    act.activation(probs[:], logits[:], ACT.Sigmoid).then_inc(S["probs_ready"], 1)

            pipeline(act, step)

            def copy_x(j, r):
                act.wait_ge(S["xtT_ready"], j + 1)
                act.activation(xT[r % 2][:], bank[r % 2][:, 0:P], ACT.Copy).then_inc(S["xT_done"], 1)

            def silu(j, r):
                act.wait_ge(S["gate_up_ready"], j + 1)
                act.activation(sge[r % 2][:], bank[2 + r % 2][:, 0:I], ACT.Silu).then_inc(S["silu_done"], 1)

            copy_x(0, 0)
            copy_x(1, 1)
            silu(0, 0)
            copy_x(2, 2)
            silu(1, 1)
            for j in range(1, BODY + 1):
                copy_x(j + 2, (j + 2) % BODY)
                silu(j + 1, (j + 1) % BODY)
            with act.Fori(BODY + 1, TILES - 2 - BODY, BODY) as j:
                for q in range(BODY):
                    copy_x(j + (q + 2), (1 + q + 2) % BODY)
                    silu(j + (q + 1), (1 + q + 1) % BODY)
            copy_x(TILES - 1, (TILES - 1) % BODY)
            silu(TILES - 2, (TILES - 2) % BODY)
            silu(TILES - 1, (TILES - 1) % BODY)

        @block.vector
        def _(dve):
            dve.wait_ge(S["iota_done"], 8)
            dve.tensor_copy(expert_iota[:], iota_i[:, 0:E])
            dve.tensor_copy(region_rows[:], iota_i[:, E:2 * E])
            dve.tensor_copy(running[:], iota_i[:, E:2 * E])
            dve.tensor_copy(dest_next[:], iota_i[:, 2 * E:2 * E + NT * K].rearrange("p (t k) -> p t k", k=K))
            dve.tensor_copy(lane[:], iota_i[:, 32:33])
            dve.tensor_copy(pad_dest[:], iota_i[:, 40:40 + E])
            dve.tensor_copy(trash_row[:], iota_i[:, 48:48 + E])
            dve.wait_ge(S["pool_const"], 12)
            dve.tensor_copy(spare_rows[:, :, D:D + 1].bitcast(I32).rearrange("p t o -> p (t o)"),
                            iota_i[:, 56:56 + SPARE_TILES]).then_inc(S["spare_ready"], 1)
            dve.tensor_copy(pad_rows[:, :, D:D + 1].bitcast(I32).rearrange("p t o -> p (t o)"), iota_i[:, 40:40 + E])
            dve.tensor_copy(tile_iota[:], iota_i[0:1, 64:64 + TILES]).then_inc(S["dve_const"], 1)
            dve.wait_ge(S["dve_const"], 1)
            dve.wait_ge(S["setup_psum"], 1)
            for i, w in enumerate((WrT, WvT, WwT, WoT)):
                dve.tensor_copy(w[:], bank[0][:, i * P:(i + 1) * P])
            dve.tensor_copy(WksT[:], bank[1][:, 0:P]).then_inc(S["setup_copied"], 1)
            dve.wait_ge(S["setup_psum"], 2)
            dve.tensor_copy(csiluT[:], bank[2][:, 0:NB]).then_inc(S["setup_copied"], 1)
            dve.wait_ge(S["setup_psum"], 3)
            mod_f = mod_sb[:].rearrange("b m d -> b (m d)")
            dve.tensor_copy(mod_f[:, 0:3 * D], bank[3][0:NB, 0:3 * D])
            dve.tensor_copy(mod_f[:, 3 * D:6 * D], bank[4][0:NB, 0:3 * D])
            dve.tensor_copy(mod_col[:, 0:2 * NB:2], bank[5][:, 0:NB])
            dve.tensor_scalar(mod_col[:, 1:2 * NB:2], bank[5][:, NB:2 * NB], 1.0, None, ALU.add)\
                .then_inc(S["setup_copied"], 1)
            dve.wait_ge(S["setup_copied"], 3)
            gates = mod_sb[:, 2:6:3, :]
            dve.tensor_scalar(sign_sb[:], gates, 0.0, 2.0, ALU.is_ge, ALU.mult)
            dve.scalar_tensor_tensor(out=mag_sb[:], in0=gates, scalar=-1.0, in1=gates, op0=ALU.mult, op1=ALU.max)\
                .then_inc(S["mod_step"], 1)
            dve.wait_ge(S["mod_step"], 1)
            dve.tensor_scalar(mag_sb[:], mag_sb[:], 0.25, None, ALU.max).then_inc(S["mod_step"], 1)
            dve.wait_ge(S["mod_step"], 2)
            dve.scalar_tensor_tensor(out=gates, in0=sign_sb[:], scalar=-1.0, in1=mag_sb[:], op0=ALU.add, op1=ALU.mult)
            dve.tensor_scalar(mod_sb[:, 4, :], mod_sb[:, 4, :], 1.0, None, ALU.add).then_inc(S["mod_ready"], 1)
            dve.wait_ge(S["setup_psum"], 4)
            dve.tensor_copy(SgT[:], bank[6][:, 0:I])
            dve.tensor_copy(SuT[:], bank[6][:, I:2 * I])
            dve.tensor_copy(SdT[:].rearrange("p m h -> p (m h)"), bank[7][:, 0:M * P])
            dve.tensor_copy(RwT[:], bank[7][:, M * P:M * P + E]).then_inc(S["setup_copied"], 1)
            dve.wait_ge(S["setup_copied"], 4)

            def scattered(b, par):
                batch = 16 * K * NT
                return (batch // 2) * b - (batch // 2) * par

            def norm_stats(src, stats, mv, var, count, s_stats, s_mv, s_var):
                for t in range(NT):
                    last = dve.bn_stats(stats[:, t, :], src(t))
                last.then_inc(s_stats, 1)
                wait_apart(dve, s_stats, count, S["dve_const"])
                for t in range(NT):
                    last = dve.bn_aggr(mv[:, t, :], stats[:, t, :])
                last.then_inc(s_mv, 1)
                dve.wait_ge(s_mv, count)
                dve.tensor_scalar(var[:], mv[:, :, 1], LN_EPS, None, ALU.add).then_inc(s_var, 1)

            def step(b, par, front, middle, back):
                f, g, h = b + 1, b, b - 1

                def mult(q):
                    n, m = q // M, q % M
                    dve.wait_ge(S["up_ready"], 4 * h + q + 1)
                    dve.wait_ge(S["silu_ready"], 4 * h + q + 1)
                    if q == 0:
                        need(dve, S["down_ready"], NC * h)
                    dve.tensor_tensor(guT[:, m, n * CH:(n + 1) * CH], sg[:, q, :], b_up[q % 2][:], ALU.mult)\
                        .then_inc(S["gu_ready"], 1)

                if front:
                    wait_apart(dve, x_loaded[1 - par], landed(f, 1 - par, 2), S["dve_const"])
                    norm_stats(lambda t: xb[1 - par][:, t, :], stats1, mv1, var1, f + 1,
                               S["stats1_done"], S["mv1_done"], S["var1_ready"])
                    need(dve, S["h1T_ready"], NC * f)
                    dve.tensor_copy(cur_col[:], mod_col[:, bass.ds(f * 2, 2)]).then_inc(S["col_ready"], 1)
                if middle:
                    dve.wait_ge(S["ss_ready"], g + 1)
                    dve.tensor_scalar(var3[:], b_small[:, SS:SS + NT], 1.0 / D, RMS_EPS, ALU.mult, ALU.add)\
                        .then_inc(S["var3_ready"], 1)
                if back:
                    dve.wait_ge(S["pos_ready"], h + 1)
                    ev = lambda a: a.rearrange("p (e t) -> p e t", e=E)
                    dve.tensor_tensor(ev(pos[:]), ev(b_small[:, PO:PO + E * NT]),
                                      running[:].unsqueeze(2).to_broadcast([P, E, NT]), ALU.add)
                    dve.tensor_tensor(tmpf[:], running[:], b_small[:, CN:CN + E], ALU.add).then_inc(S["pos_done"], 1)
                    dve.wait_ge(S["pos_done"], h + 1)
                    dve.tensor_copy(running[:], tmpf[:])
                    pv = pos[:].rearrange("p (e t) -> p t e", e=E)
                    for k in range(K):
                        last = dve.tensor_tensor(prod[:, k], onehot[:, k], pv, ALU.mult)
                    last.then_inc(S["prod_done"], 1)
                    dve.wait_ge(S["prod_done"], h + 1)
                    dve.tensor_reduce(slotf[:], prod[:].rearrange("p k t e -> p (k t) e"), AX_X, ALU.add)\
                        .then_inc(S["slotf_done"], 1)
                    dve.wait_ge(S["slotf_done"], h + 1)
                    need(dve, rows_scattered[par], scattered(b, par))
                    dve.tensor_copy(slots[:], slotf[:]).then_inc(S["slots_ready"], 1)
                if middle:
                    dve.wait_ge(S["rstd3_ready"], g + 1)
                    for t in range(NT):
                        if t % TC == 0:
                            dve.wait_ge(S["wo_ready"], NC * g + t // TC + 1)
                        last = dve.scalar_tensor_tensor(
                            out=resid_tiles(g, t, 1), in0=b_O[t // TC][:, (t % TC) * P:(t % TC + 1) * P],
                            scalar=rstd3[:, t:t + 1], in1=xb[par][:, t, :], op0=ALU.mult, op1=ALU.add)
                    last.then_inc(S["x1_ready"], 1)
                    if back:
                        mult(0)
                    wait_apart(dve, S["x1_ready"], g + 1, S["dve_const"])
                    norm_stats(lambda t: resid_tiles(g, t, 1), stats2, mv2, var2, g + 1,
                               S["stats2_done"], S["mv2_done"], S["var2_ready"])
                elif back:
                    mult(0)
                if back:
                    mult(1)
                    mult(2)
                if front:
                    dve.wait_ge(S["mod_row_loaded"], 16)
                    need(dve, S["wo_ready"], NC * f)
                    dve.tensor_tensor(Wo_b[:], WoT[:], mod_at(f, 0), ALU.mult).then_inc(S["wo_scaled"], 1)
                    dve.wait_ge(S["rstd1_ready"], f + 1)
                    need(dve, S["xT_ready"], NC * f)
                    for t in range(NT):
                        last = dve.tensor_scalar(xn1[:, t, :], xb[1 - par][:, t, :], mv1[:, t, 0:1], rstd1[:, t:t + 1],
                                                 ALU.subtract, ALU.mult)
                    last.then_inc(S["xn1_ready"], 1)
                if back:
                    need(dve, S["down_ready"], NC * h)
                    for m in range(M):
                        last = dve.tensor_tensor(Sd_b[:, m, :], SdT[:, m, :], mod_at(h, 3), ALU.mult)
                    last.then_inc(S["sd_scaled"], 1)
                    mult(3)
                if middle:
                    dve.wait_ge(S["rstd2_ready"], g + 1)
                    for t in range(NT):
                        last = dve.tensor_scalar(xn2[:, t, :], resid_tiles(g, t, 1), mv2[:, t, 0:1], rstd2[:, t:t + 1],
                                                 ALU.subtract, ALU.mult)
                    last.then_inc(S["xn2_done"], 1)
                    dve.wait_ge(S["xn2_done"], g + 1)
                    over = lambda a: a.unsqueeze(1).to_broadcast([P, NT, D])
                    dve.tensor_tensor(xn2[:], xn2[:], over(mod_at(g, 2)), ALU.mult).then_inc(S["h2_scaled"], 1)
                    dve.wait_ge(S["h2_scaled"], g + 1)
                    need(dve, rows_scattered[par], scattered(b, par))
                    dve.tensor_tensor(rows[par][:, :, 0, 0:D], xn2[:], over(mod_at(g, 1)), ALU.add)\
                        .then_inc(S["h2_ready"], 1)
                if front:
                    for n in range(NC):
                        at = slice(n * CH, (n + 1) * CH)
                        dve.wait_ge(S["w_done"], NC * f + n + 1)
                        dve.tensor_scalar(wsig[:, at], wsig[:, at], 0.99, None, ALU.mult).then_inc(S["decay_done"], 1)
                        dve.wait_ge(S["ks_done"], NC * f + n + 1)
                        dve.wait_ge(S["v_ready"], NC * f + n + 1)
                        dve.tensor_tensor(ksT[:, at], ksT[:, at], b_proj[1][:], ALU.mult).then_inc(S["kv_done"], 1)
                        dve.wait_ge(S["decay_done"], NC * f + n + 1)
                        dve.wait_ge(S["kv_done"], NC * f + n + 1)
                        dve.tensor_tensor_scan(stateT[:, at], wsig[:, at], ksT[:, at],
                                               0.0 if n == 0 else stateT[:, n * CH - 1:n * CH], ALU.mult, ALU.add)\
                            .then_inc(S["state_done"], 1)
                        dve.wait_ge(S["state_done"], NC * f + n + 1)
                        if n == 0:
                            need(dve, S["wo_ready"], NC * f)
                            need(dve, S["sq_ready"], NC * f)
                        dve.tensor_tensor(outT[:, at], stateT[:, at], rT[:, at], ALU.mult).then_inc(S["out_ready"], 1)
                if back:
                    for n in range(NC):
                        dve.wait_ge(S["down_ready"], NC * h + n + 1)
                        tiles = resid_tiles(h, n * TC, TC)
                        dve.tensor_tensor(tiles, b_O[n][:], tiles, ALU.add).then_inc(S["base_ready"], 1)
                if middle:
                    dve.wait_ge(S["logits_psum"], g + 1)
                    dve.tensor_tensor(logits[:], b_small[:, LG:LG + NT * E].rearrange("p (t e) -> p t e", e=E),
                                      bias_row[:].unsqueeze(1).to_broadcast([P, NT, E]), ALU.add)\
                        .then_inc(S["logits_ready"], 1)
                    wait_apart(dve, S["probs_ready"], g + 1, S["dve_const"])
                    for t in range(NT):
                        last = dve.max(top[:, t, :], probs[:, t, :])
                    last.then_inc(S["top_done"], 1)
                    wait_apart(dve, S["top_done"], g + 1, S["dve_const"])
                    for t in range(NT):
                        last = dve.max_index(topi[:, t, :], top[:, t, :], probs[:, t, :])
                    last.then_inc(S["topi_done"], 1)
                    dve.tensor_tensor(den[:], top[:, :, 0], top[:, :, 1], ALU.add).then_inc(S["den_done"], 1)
                    dve.wait_ge(S["topi_done"], g + 1)
                    dve.tensor_copy(topf[:], topi[:, :, 0:K].rearrange("p t k -> p k t")).then_inc(S["topf_done"], 1)
                    dve.wait_ge(S["den_done"], g + 1)
                    dve.reciprocal(rden[:], den[:]).then_inc(S["rden_done"], 1)
                    dve.wait_ge(S["topf_done"], g + 1)
                    for k in range(K):
                        last = dve.tensor_tensor(onehot[:, k], topf[:, k, :].unsqueeze(2).to_broadcast([P, NT, E]),
                                                 expert_iota[:].unsqueeze(1).to_broadcast([P, NT, E]), ALU.is_equal)
                    last.then_inc(S["onehot_done"], 1)
                    dve.wait_ge(S["rden_done"], g + 1)
                    dve.tensor_tensor(rows[par][:, :, :, D + 1], top[:, :, 0:K],
                                      rden[:].unsqueeze(2).to_broadcast([P, NT, K]), ALU.mult)
                    dve.tensor_copy(rows[par][:, :, :, D].bitcast(I32), dest_next[:]).then_inc(S["meta_ready"], 1)
                    dve.wait_ge(S["onehot_done"], g + 1)
                    need(dve, S["pos_ready"], g)
                    dve.tensor_tensor(picks[:].rearrange("p (e t) -> p t e", e=E), onehot[:, 0], onehot[:, 1], ALU.add)\
                        .then_inc(S["picks_done"], 1)
                    dve.wait_ge(S["picks_done"], g + 1)
                    dve.tensor_tensor_scan(picks_sum[:], tile_start[:], picks[:], 0.0, ALU.mult, ALU.add)\
                        .then_inc(S["picks_sum_done"], 1)
                    dve.wait_ge(S["picks_sum_done"], g + 1)
                    dve.tensor_tensor(picks_before[:], picks_sum[:], picks[:], ALU.subtract).then_inc(S["picks_ready"], 1)
                    dve.wait_ge(S["meta_ready"], g + 1)
                    dve.tensor_scalar(dest_next[:], dest_next[:], float(K * T), None, ALU.add)

            pipeline(dve, step)

            count = [0]

            def then(instruction):
                count[0] += 1
                instruction.then_inc(S["table_step"], 1)
                dve.wait_ge(S["table_step"], count[0])

            then(dve.tensor_tensor(counts[:], tmpf[:], region_rows[:], ALU.subtract))
            then(dve.tensor_scalar(tmpi[:], counts[:], float(P - 1), None, ALU.add))
            then(dve.tensor_scalar(tilesi[:], tmpi[:], 7, None, ALU.arith_shift_right))
            then(dve.tensor_copy(tilesf[:], tilesi[:]))
            then(dve.tensor_tensor_scan(ends[:], ones_e[:], tilesf[:], 0.0, ALU.mult, ALU.add))
            then(dve.tensor_scalar(skip[:], tilesf[:], -1.0, float(CAP // P), ALU.mult, ALU.add))
            over_e = lambda a: a.unsqueeze(1).to_broadcast([1, TILES, E])
            then(dve.tensor_tensor(passed[:], tile_iota[:].unsqueeze(2).to_broadcast([1, TILES, E]),
                                   over_e(ends[0:1, :]), ALU.is_ge))
            then(dve.tensor_tensor(passed_skip[:], passed[:], over_e(skip[0:1, :]), ALU.mult))
            dve.tensor_reduce(tab_f[:, 0, :], passed[:], AX_X, ALU.add)
            then(dve.tensor_reduce(tab_f[:, 1, :], passed_skip[:], AX_X, ALU.add))
            then(dve.tensor_tensor(tab_g[:, 1, :], tab_f[:, 1, :], tile_iota[:], ALU.add))
            dve.tensor_scalar(tab[:, TILES:2 * TILES], tab_g[:, 1, :], float(P), None, ALU.mult)
            dve.tensor_scalar(tab[:, 0:TILES], tab_f[:, 0, :], float(E - 1), float(WE), ALU.min, ALU.mult).then_inc(S["table_ready"], 1)
            then(dve.tensor_copy(tmpi[:], counts[:]))
            then(dve.tensor_scalar(modi[:], tmpi[:], P - 1, None, ALU.bitwise_and))
            then(dve.tensor_copy(modf[:], modi[:]))
            then(dve.tensor_scalar(padv[:], modf[:], lane[:, 0:1], float(P), ALU.add, ALU.is_lt))
            then(dve.scalar_tensor_tensor(out=padd[:], in0=modf[:], scalar=0.0, in1=padv[:], op0=ALU.is_gt, op1=ALU.mult))
            then(dve.tensor_scalar(padr[:], tmpf[:], lane[:, 0:1], None, ALU.add))
            then(dve.tensor_tensor(padr[:], padr[:], trash_row[:], ALU.subtract))
            then(dve.tensor_tensor(padr[:], padr[:], padd[:], ALU.mult))
            dve.tensor_tensor(pad_slot[:], padr[:], trash_row[:], ALU.add).then_inc(S["pad_ready"], 1)

            def mult_e(j, r):
                dve.wait_ge(S["silu_done"], j + 1)
                dve.tensor_tensor(pe_in[r % 2][:], sge[r % 2][:], bank[2 + r % 2][:, I:2 * I], ALU.mult)\
                    .then_inc(S["gu_done"], 1)

            def copy_gu(j, r):
                dve.wait_ge(S["guT_psum"], j + 1)
                dve.tensor_copy(guTe[r % 2][:], bank[6 + r % 2][:, 0:I]).then_inc(S["guT_done"], 1)

            def copy_meta(j, r):
                dve.wait_ge(xt_loaded[r], landed(j, r, XR))
                need(dve, y_scattered[r], (16 // XR) * j - (16 // XR) * r)
                dve.tensor_copy(meta[r][:], xt[r][:, D:D + 2]).then_inc(S["meta_done"], 1)

            def scale_y(j, r):
                dve.wait_ge(S["y_psum"], j + 1)
                dve.wait_ge(S["meta_done"], j + 1)
                dve.tensor_scalar(ye[r][:], bank[4 + r % 2][:, 0:D], meta[r][:, 1:2], None, ALU.mult)\
                    .then_inc(S["y_done"], 1)

            copy_meta(0, 0)
            mult_e(0, 0)
            copy_meta(1, 1)
            mult_e(1, 1)
            copy_gu(0, 0)

            def step_e(j, r, gates=True):
                if gates:
                    copy_meta(j + 1, (r + 1) % BODY)
                    mult_e(j + 1, (r + 1) % BODY)
                copy_gu(j, r)
                scale_y(j - 1, (r - 1) % BODY)

            for j in range(1, BODY + 1):
                step_e(j, j % BODY)
            with dve.Fori(BODY + 1, TILES - 2 - BODY, BODY) as j:
                for q in range(BODY):
                    step_e(j + q, (1 + q) % BODY)
            for j in range(TILES - 3, TILES):
                step_e(j, j % BODY, gates=j + 1 < TILES)
            scale_y(TILES - 1, (TILES - 1) % BODY)

            def combine(b, n, r, i):
                dve.wait_ge(yb_loaded[r], 16 * (b + 1))
                dve.tensor_tensor(acc[r], yb[r][:, :, 0, :], yb[r][:, :, 1, :], ALU.add).then_inc(S["y_sum"], 1)
                dve.wait_ge(S["y_sum"], i + 1)
                dve.tensor_tensor(acc[r], acc[r], mod_at(b, 3).unsqueeze(1).to_broadcast([P, TC, D]), ALU.mult)\
                    .then_inc(S["y_gated"], 1)
                dve.wait_ge(S["y_gated"], i + 1)
                need(dve, out_stored[r], 16 * b)
                dve.tensor_tensor(fin[r].rearrange("p t d -> p (t d)"), acc[r].rearrange("p t d -> p (t d)"),
                                  resid_tiles(b, n * TC, TC), ALU.add).then_inc(S["fin_ready"], 1)

            for n in range(NC):
                combine(0, n, n, n)
            with dve.Fori(1, NB) as b:
                for n in range(NC):
                    combine(b, n, n, b * NC + n)


_INS = ["L0_attn_x", "L0_attn_Wr", "L0_attn_Wk", "L0_attn_Wv", "L0_attn_Ww", "L0_attn_Wo", "L0_ffn_shared_gate",
        "L0_ffn_shared_up", "L0_ffn_shared_down", "L0_ffn_gate_w", "L0_ffn_up_w", "L0_ffn_down_w",
        "L0_ffn_router_w", "L0_ffn_routing_bias", "L0_c", "L0_wmod"]


def kernel(**inputs):
    import numpy as np
    import concourse.bacc as bacc
    from concourse.bass_utils import run_bass_kernel_spmd

    nc = bacc.Bacc("TRN2", target_bir_lowering=False, num_devices=1)
    arrays, args = {}, []
    for name in _INS:
        a = np.ascontiguousarray(inputs[name])
        arrays[f"in_{name}"] = a
        args.append(nc.dram_tensor(f"in_{name}", a.shape, mybir.dt.from_np(a.dtype), kind="ExternalInput").ap())
    out = nc.dram_tensor("out_0", inputs["L0_attn_x"].shape, F32, kind="ExternalOutput").ap()
    build(nc, *args, out)
    r = run_bass_kernel_spmd(nc, [arrays], core_ids=[0])
    return r.results[0]["out_0"]
```

```python
from contextlib import ExitStack

import concourse.bass as bass
from concourse import mybir

ALU = mybir.AluOpType
ACT = mybir.ActivationFunctionType
F32 = mybir.dt.float32
BF16 = mybir.dt.bfloat16
I32 = mybir.dt.int32
U32 = mybir.dt.uint32
AX_X = mybir.AxisListType.X

P = 128


def need(engine, semaphore, count):
    if isinstance(count, int) and count <= 0:
        return
    engine.wait_ge(semaphore, count)


def wait_apart(engine, semaphore, count, met):
    if not isinstance(count, int):
        count = engine.to_reg(count)
    engine.wait_ge(met, 1)
    engine.wait_ge(semaphore, count)


def landed(k, slot, ring, each=16):
    return (each // ring) * k + (each - (each // ring) * slot)


def build(nc, x, Wr, Wk, Wv, Ww, Wo, shared_gate, shared_up, shared_down, gate_w, up_w, down_w,
          router_w, routing_bias, c, wmod, out):
    NB, T, D = x.shape
    NH = 16
    HD = D // NH
    E, _, I = gate_w.shape
    M = I // P
    K = 2
    NT = T // P
    CH = 512
    NC = T // CH
    TC = CH // P
    TOKENS = NB * T
    TR = 2 * P
    HB = TR // P
    REGION = TOKENS + TR
    BODY = 4
    TILES = -(-(TOKENS * K // TR + E - 1) // BODY) * BODY
    SPARE_TILES = TILES - TOKENS * K // TR
    SPARE0 = E * REGION
    ROWS = SPARE0 + SPARE_TILES * TR
    W = 132
    YPAD0 = TOKENS * K
    YROWS = YPAD0 + (E + SPARE_TILES) * TR
    LN_EPS = 1e-5
    RMS_EPS = 1.1920928955078125e-07

    with ExitStack() as ctx:
        def sb(name, shape, dt=F32):
            return ctx.enter_context(nc.sbuf_tensor(name, shape, dt))

        def sem(name):
            return ctx.enter_context(nc.semaphore(name))

        bank = [ctx.enter_context(nc.psum_tensor(f"bank{i}", [P, 512], F32)) for i in range(8)]

        expert_rows = nc.dram_tensor("expert_rows", (ROWS, W), F32).ap()
        result_rows = nc.dram_tensor("result_rows", (YROWS, D), F32).ap()
        mod_rows = nc.dram_tensor("mod_rows", (NB, 4 * D), F32).ap()

        ident = sb("ident", [P, P])
        head_ones = sb("head_ones", [P, P])
        before = sb("before", [P, P], BF16)
        ones_bf = sb("ones_bf", [P, P], BF16)
        ones_col = sb("ones_col", [P, 2])
        minus_half = sb("minus_half", [P, NT])
        tile_start = sb("tile_start", [P, E * NT])
        iota_i = sb("iota_i", [P, 256], I32)
        expert_iota = sb("expert_iota", [P, E])
        region_rows = sb("region_rows", [P, E])
        running = sb("running", [P, E])
        dest_next = sb("dest_next", [P, NT, K])
        rraw = sb("rraw", [E, P])
        craw = sb("craw", [NB, D])
        bias_row = sb("bias_row", [P, E])
        WrT = sb("WrT", [P, P])
        WvT = sb("WvT", [P, P])
        WwT = sb("WwT", [P, P])
        WksT = sb("WksT", [P, P])
        WoT = sb("WoT", [P, P])
        Wo_b = sb("Wo_b", [P, P])
        SgT = sb("SgT", [P, I])
        SuT = sb("SuT", [P, I])
        SdT = sb("SdT", [P, M, P])
        Sd_b = sb("Sd_b", [P, M, P])
        RwT = sb("RwT", [P, E])
        WE = 2 * I + M * D
        Wexp = sb("Wexp", [P, E * WE])

        csilu = sb("csilu", [NB, D])
        csiluT = sb("csiluT", [P, NB])
        mod_sb = sb("mod_sb", [NB, 6, D])
        sign_sb = sb("sign_sb", [NB, 2, D])
        mag_sb = sb("mag_sb", [NB, 2, D])
        mod_col = sb("mod_col", [P, NB * 2])
        cur_col = sb("cur_col", [P, 2])
        mod_row = sb("mod_row", [P, NB * 4 * D])

        xb = [sb(f"xb{i}", [P, NT, D]) for i in range(2)]
        stats1 = sb("stats1", [P, NT, 6])
        mv1 = sb("mv1", [P, NT, 2])
        var1 = sb("var1", [P, NT])
        rstd1 = sb("rstd1", [P, NT])
        nmean1 = sb("nmean1", [P, NT])
        shift1 = sb("shift1", [P, NT])
        xn1 = sb("xn1", [P, NT, D])
        h1T = sb("h1T", [P, T])
        rT = sb("rT", [P, T])
        wsig = sb("wsig", [P, T])
        ksT = sb("ksT", [P, T])
        stateT = sb("stateT", [P, T])
        outT = sb("outT", [P, T])
        sqT = sb("sqT", [P, T])
        wraw = sqT[:, 0:5 * P].rearrange("p (i n) -> p i n", i=5)
        sgraw = outT[:, 0:I].rearrange("p (m n) -> p m n", m=M)
        suraw = outT[:, I:2 * I].rearrange("p (m n) -> p m n", m=M)
        sdraw = outT[:, 2 * I:3 * I]
        wmod_sb = stateT[:, 0:6 * D]
        resid = sb("resid", [P, NB * NT * D])
        var3 = sb("var3", [P, NT])
        rstd3 = sb("rstd3", [P, NT])
        stats2 = sb("stats2", [P, NT, 6])
        mv2 = sb("mv2", [P, NT, 2])
        var2 = sb("var2", [P, NT])
        rstd2 = sb("rstd2", [P, NT])
        nmean2 = sb("nmean2", [P, NT])
        shift2 = sb("shift2", [P, NT])
        xn2 = sb("xn2", [P, NT, D])
        rows = [sb(f"rows{i}", [P, NT, K, W]) for i in range(2)]
        h2T = [sb(f"h2T{i}", [P, T]) for i in range(2)]
        logits = sb("logits", [P, NT, E])
        probs = sb("probs", [P, NT, E])
        top = sb("top", [P, NT, 8])
        topi = sb("topi", [P, NT, 8], U32)
        topf = sb("topf", [P, K, NT])
        onehot = sb("onehot", [P, K, NT, E])
        picks = sb("picks", [P, E * NT], BF16)
        picks_sum = sb("picks_sum", [P, E * NT], BF16)
        picks_before = sb("picks_before", [P, E * NT], BF16)
        den = sb("den", [P, NT])
        rden = sb("rden", [P, NT])
        pos = sb("pos", [P, E * NT])
        prod = sb("prod", [P, K, NT, E])
        slotf = sb("slotf", [P, K * NT])
        slots = sb("slots", [P, K * NT], I32)
        sg = sb("sg", [P, 4, CH])
        guT = sb("guT", [P, M, T])
        counts = sb("counts", [P, E])
        tmpf = sb("tmpf", [P, E])
        tmpi = sb("tmpi", [P, E], I32)
        tilesi = sb("tilesi", [P, E], I32)
        tilesf = sb("tilesf", [P, E])
        ends = sb("ends", [P, E])
        skip = sb("skip", [P, E])
        ones_e = sb("ones_e", [P, E])
        touched = sb("touched", [1, 1])
        pad_rows = sb("pad_rows", [P, E, HB, W])
        spare_rows = sb("spare_rows", [P, SPARE_TILES * HB, W])
        tile_iota = sb("tile_iota", [1, TILES])
        passed = guT[0:1].rearrange("a m n -> a (m n)")[:, 0:TILES * E].rearrange("a (j e) -> a j e", e=E)
        passed_skip = sg[0:1].rearrange("a m n -> a (m n)")[:, 0:TILES * E].rearrange("a (j e) -> a j e", e=E)
        tab_f = sb("tab_f", [1, 2, TILES])
        tab_g = sb("tab_g", [1, 2, TILES])
        tab = sb("tab", [1, 2 * TILES + E], I32)
        XR = 4
        xt = [sb(f"xt{i}", [P, HB, W]) for i in range(XR)]
        meta = [sb(f"meta{i}", [P, HB, 2]) for i in range(XR)]
        halves = lambda a: [a[:, 0:CH], a[:, CH:2 * CH]]
        xT = [ksT[:, i * TR:(i + 1) * TR] for i in range(2)]
        wc = halves(wsig)
        sge = halves(outT)
        guTe = [guT[:, 0, i * M * TR:(i + 1) * M * TR].rearrange("p (m t) -> p m t", m=M) for i in range(2)]
        ye = [stateT[:, i * TR:(i + 1) * TR].rearrange("p (n d) -> p n d", n=HB) for i in range(XR)]
        yb = [rows[i][:].rearrange("p t k w -> p (t k w)")[:, 0:CH * K].rearrange("p (t k d) -> p t k d", k=K, d=D)
              for i in range(2)]
        acc = [h1T[:, i * CH:(i + 1) * CH].rearrange("p (t d) -> p t d", d=D) for i in range(2)]
        fin = [rT[:, i * CH:(i + 1) * CH].rearrange("p (t d) -> p t d", d=D) for i in range(2)]

        S = {}
        for name in (
            "attn_w_loaded", "mod_w_loaded", "ffn_w_loaded", "expert_w_loaded", "mod_stored", "mod_row_loaded",
            "pool_const", "ident_ready", "iota_done", "dve_const", "setup_psum", "setup_copied", "csilu_ready", "mod_step",
            "mod_ready",
            "stats1_done", "mv1_done", "var1_ready", "rstd1_ready", "norm1_ready", "col_ready", "xn1_ready",
            "xT_ready", "h1T_ready", "r_ready", "w_ready", "ks_ready", "v_ready", "r_done", "w_done", "ks_done",
            "kv_done", "state_done", "out_ready", "sq_ready",
            "small_ready", "var3_ready", "rstd3_ready", "wo_scaled", "wo_ready", "x1_ready", "stats2_done", "mv2_done",
            "var2_ready", "rstd2_ready", "norm2_ready", "xn2_done", "h2_scaled", "h2_ready", "h2xT_ready", "h2T_ready",
            "rows2_ready", "logits_ready", "probs_ready", "top_done", "topi_done", "topf_done", "onehot_done",
            "picks_done", "picks_sum_done", "picks_ready", "den_done", "rden_done", "meta_ready",
            "pos_ready", "pos_done", "prod_done", "slotf_done", "slots_ready", 
            "gate_ready", "up_ready", "silu_ready", "gu_ready", "sd_scaled", "down_ready", "base_ready", "touched",
            "table_step", "ends_ready", "table_ready", "spare_ready", "spare_stored", "pads_stored",
            "xtT_ready", "xT_done", "wc_done", "e_gate_ready", "e_up_ready", "silu_done", "meta_done", "gu_done",
            "y_psum", "y_done", 
            "y_sum", "y_gated", "fin_ready", 
        ):
            S[name] = sem(name)
        x_loaded = [sem(f"x_loaded{i}") for i in range(2)]
        rows_scattered = [sem(f"rows_scattered{i}") for i in range(2)]
        xt_loaded = [sem(f"xt_loaded{i}") for i in range(XR)]
        y_scattered = [sem(f"y_scattered{i}") for i in range(XR)]
        yb_loaded = [sem(f"yb_loaded{i}") for i in range(2)]
        out_stored = [sem(f"out_stored{i}") for i in range(2)]

        x_v = x.rearrange("b (t p) d -> p (b t) d", p=P)
        res_v = resid[:, :]
        out_v = out.rearrange("b (t p) d -> p (b t) d", p=P)
        y_v = result_rows[0:TOKENS * K, :].rearrange("(n p k) d -> p n k d", p=P, k=K)

        def mod_at(b, which):
            return mod_row[:, bass.ds((b * 4 + which) * D, D)]

        def resid_tiles(b, t, n):
            return res_v[:, bass.ds((b * NT + t) * D, n * D)]

        b_T, b_small = bank[0], bank[1]
        b_proj = [bank[2], bank[3]]
        b_O = [bank[4], bank[5]]
        b_gate, b_up = bank[6], bank[7]
        SS, LG, PO, CN = 0, 8, 8 + NT * E, 8 + 2 * NT * E

        e_x = [bank[0], bank[1]]
        e_gate, e_up = [bank[2], bank[3]], [bank[4], bank[5]]
        e_y = [bank[6], bank[7]]

        def weights_of(j, engine):
            return nc.values_load_multi_w_load_instructions(
                tab[0:1, bass.ds(j, 1)], engines=[engine], min_val=0, max_val=(E - 1) * WE,
                skip_runtime_bounds_check_because="the table's values are clamped")[1][0]

        block = ctx.enter_context(nc.Block())

        def pipeline(eng, step):
            step(-1, 1, True, True, False, False)
            step(0, 0, True, True, True, False)
            step(1, 1, True, True, True, True)
            with eng.Fori(2, NB - 3, 2) as b:
                step(b, 0, True, True, True, True)
                step(b + 1, 1, True, True, True, True)
            step(NB - 2, 0, False, True, True, True)
            step(NB - 1, 1, False, False, True, True)
            step(NB, 0, False, False, False, True)

        @block.sync
        def _(sp):
            sp.dma_start(craw[:], c).then_inc(S["mod_w_loaded"], 16)
            sp.dma_start(wmod_sb, wmod).then_inc(S["mod_w_loaded"], 16)
            for i, w in enumerate((Wr, Wk, Wv, Ww, Wo)):
                sp.dma_start(wraw[:, i, :], w).then_inc(S["attn_w_loaded"], 16)
            for b in range(2):
                sp.dma_start(xb[b][:], x_v[:, b * NT:(b + 1) * NT, :]).then_inc(x_loaded[b], 16)
            sp.dma_start(sgraw, shared_gate.rearrange("(m p) h -> p m h", p=P)).then_inc(S["ffn_w_loaded"], 16)
            sp.dma_start(suraw, shared_up.rearrange("(m p) h -> p m h", p=P)).then_inc(S["ffn_w_loaded"], 16)
            sp.dma_start(sdraw, shared_down).then_inc(S["ffn_w_loaded"], 16)
            sp.dma_start(rraw[:], router_w).then_inc(S["ffn_w_loaded"], 16)
            sp.dma_start(bias_row[:], routing_bias.rearrange("(a e) -> a e", a=1).to_broadcast([P, E]))\
                .then_inc(S["ffn_w_loaded"], 16)
            sp.wait_ge(S["mod_ready"], 1)
            sp.dma_start(mod_rows, mod_sb[:, 2:6, :].rearrange("b m d -> b (m d)")).then_inc(S["mod_stored"], 16)
            sp.wait_ge(S["mod_stored"], 16)
            sp.dma_start(mod_row[:], mod_rows.rearrange("b n -> (b n)").rearrange("(a n) -> a n", a=1)
                         .to_broadcast([P, NB * 4 * D])).then_inc(S["mod_row_loaded"], 16)
            for e in range(E):
                wg = Wexp[:, e * WE:(e + 1) * WE]
                sp.dma_start(wg[:, 0:I], gate_w[e]).then_inc(S["expert_w_loaded"], 16)
                sp.dma_start(wg[:, I:2 * I], up_w[e]).then_inc(S["expert_w_loaded"], 16)
                sp.dma_start(wg[:, 2 * I:WE].rearrange("p (m h) -> p m h", m=M),
                             down_w[e].rearrange("(m p) h -> p m h", p=P)).then_inc(S["expert_w_loaded"], 16)
            sp.wait_ge(S["spare_ready"], 1)
            sp.dma_start(expert_rows[SPARE0:ROWS, :].rearrange("(n p) w -> p n w", p=P), spare_rows[:])\
                .then_inc(S["spare_stored"], 16)

            def load_x(b, par):
                sp.wait_ge(S["x1_ready"], b - 1)
                sp.dma_start(xb[par][:], x_v[:, bass.ds(b * NT, NT), :]).then_inc(x_loaded[par], 16)

            with sp.Fori(2, NB - 1, 2) as b:
                load_x(b, 0)
                load_x(b + 1, 1)

            def load_tile(j, r):
                first = sp.value_load(tab[0:1, bass.ds(TILES + j, 1)], min_val=0, max_val=SPARE0 + (SPARE_TILES - 1) * TR)
                need(sp, S["xtT_ready"], j - XR + 1)
                need(sp, S["meta_done"], j - XR + 1)
                sp.dma_start(xt[r][:], expert_rows[bass.ds(first, TR), :].rearrange("(p n) w -> p n w", n=HB)).then_inc(xt_loaded[r], 16)

            sp.wait_ge(S["ends_ready"], 1)
            for e in range(E):
                end = sp.value_load(tab[0:1, 2 * TILES + e:2 * TILES + e + 1], min_val=e * REGION,
                                    max_val=e * REGION + TOKENS)
                sp.dma_start(expert_rows[bass.ds(end, TR), :].rearrange("(p n) w -> p n w", n=HB), pad_rows[:, e])\
                    .then_inc(S["pads_stored"], 16)
            sp.wait_ge(S["table_ready"], 1)
            for i in range(2):
                sp.wait_ge(rows_scattered[i], 16 * NT * K * NB // 2)
            sp.wait_ge(S["pads_stored"], 16 * E)
            sp.wait_ge(S["spare_stored"], 16)
            for j in range(XR):
                load_tile(j, j)
            with sp.Fori(XR, TILES - XR + 1, XR) as j:
                for r in range(XR):
                    load_tile(j + r, r)

            def load_y(n, r):
                need(sp, S["y_sum"], n - 1)
                sp.dma_start(yb[r], y_v[:, bass.ds(n * TC, TC), :, :]).then_inc(yb_loaded[r], 16)

            def store(n, r):
                sp.wait_ge(S["fin_ready"], n + 1)
                sp.dma_start(out_v[:, bass.ds(n * TC, TC), :], fin[r]).then_inc(out_stored[r], 16)

            for r in range(XR):
                sp.wait_ge(y_scattered[r], 16 * HB * TILES // XR)
            load_y(0, 0)
            load_y(1, 1)
            with sp.Fori(0, NB * NC - 3, 2) as n:
                for r in range(2):
                    load_y(n + 2 + r, r)
                    store(n + r, r)
            for n in range(NB * NC - 2, NB * NC):
                store(n, n % 2)
            for r in range(2):
                sp.wait_ge(out_stored[r], 16 * NB * NC // 2)

        @block.gpsimd
        def _(pool):
            pool.memset(ident[:], 0.0).then_inc(S["pool_const"], 1)
            pool.memset(head_ones[:], 1.0).then_inc(S["pool_const"], 1)
            pool.memset(before[:], 1.0).then_inc(S["pool_const"], 1)
            pool.memset(ones_bf[:], 1.0).then_inc(S["pool_const"], 1)
            pool.memset(ones_col[:], 1.0).then_inc(S["pool_const"], 1)
            pool.memset(minus_half[:], -0.5).then_inc(S["pool_const"], 1)
            pool.memset(pad_rows[:], 0.0).then_inc(S["pool_const"], 1)
            pool.memset(spare_rows[:], 0.0).then_inc(S["pool_const"], 1)
            for i in range(2):
                pool.memset(rows[i][:, :, :, D:W], 0.0).then_inc(S["pool_const"], 1)
            pool.memset(tile_start[:], 1.0).then_inc(S["pool_const"], 1)
            pool.memset(ones_e[:], 1.0).then_inc(S["pool_const"], 1)
            pool.wait_ge(S["pool_const"], 12)
            pool.affine_select(out=ident[:], in_=ident[:], compare_op=ALU.not_equal, fill=1.0, base=0,
                               pattern=[[-1, P]], channel_multiplier=1).then_inc(S["ident_ready"], 1)
            hv = head_ones[:].rearrange("p (g r) -> p g r", r=HD)
            pool.affine_select(out=hv, in_=hv, compare_op=ALU.is_ge, fill=0.0, base=0,
                               pattern=[[-HD, NH], [0, HD]], channel_multiplier=1).then_inc(S["ident_ready"], 1)
            pool.affine_select(out=before[:], in_=before[:], compare_op=ALU.is_gt, fill=0.0, base=0,
                               pattern=[[1, P]], channel_multiplier=-1).then_inc(S["ident_ready"], 1)
            tv = tile_start[:].rearrange("p (e t) -> p e t", e=E)
            pool.affine_select(out=tv, in_=tv, compare_op=ALU.not_equal, fill=0.0, base=0,
                               pattern=[[0, E], [1, NT]], channel_multiplier=0).then_inc(S["ident_ready"], 1)
            pool.wait_ge(S["ident_ready"], 4)
            pool.affine_select(out=hv, in_=hv, compare_op=ALU.is_ge, fill=0.0, base=HD - 1,
                               pattern=[[HD, NH], [0, HD]], channel_multiplier=-1).then_inc(S["ident_ready"], 1)
            iotas = [
                (iota_i[:, 0:E], [[1, E]], 0, 0),
                (iota_i[:, E:2 * E], [[REGION, E]], 0, 0),
                (iota_i[:, 2 * E:2 * E + NT * K], [[K * P, NT], [1, K]], 0, K),
                (iota_i[:, 32:32 + E * HB], [[P, E * HB]], YPAD0, 1),
                (iota_i[:, 64:64 + SPARE_TILES * HB], [[P, SPARE_TILES * HB]], YPAD0 + E * TR, 1),
                (iota_i[0:1, 96:96 + TILES], [[1, TILES]], 0, 0),
            ]
            for o, pattern, base, cm in iotas:
                pool.iota(o, pattern=pattern, base=base, channel_multiplier=cm).then_inc(S["iota_done"], 1)

            def power(out_, in_, ready, b, done):
                pool.wait_ge(ready, b + 1)
                pool.tensor_tensor(out_[:], in_[:], minus_half[:], ALU.pow).then_inc(done, 1)

            def norm(rstd, var, nmean, shift, ready, b, rstd_done, done):
                power(rstd, var, ready, b, rstd_done)
                pool.wait_ge(rstd_done, b + 1)
                pool.tensor_tensor(shift[:], nmean[:], rstd[:], ALU.mult).then_inc(done, 1)

            def norm1(b):
                norm(rstd1, var1, nmean1, shift1, S["var1_ready"], b, S["rstd1_ready"], S["norm1_ready"])

            def scatter(b, par, columns):
                for q in columns:
                    pool.indirect_dma_start(
                        expert_rows, bass.IndirectOffsetOnAxis(ap=slots[:, q:q + 1], axis=0),
                        rows[par][:, q % NT, q // NT, :], None).then_inc(rows_scattered[par], 16)

            def step(b, par, early, front, middle, back):
                if back:
                    wait_apart(pool, S["slots_ready"], b, S["pool_const"])
                    scatter(b - 1, 1 - par, range(0, 4))
                if middle:
                    norm(rstd2, var2, nmean2, shift2, S["var2_ready"], b, S["rstd2_ready"], S["norm2_ready"])
                if back:
                    scatter(b - 1, 1 - par, range(4, 7))
                if early:
                    norm1(b + 2)
                if back:
                    scatter(b - 1, 1 - par, range(7, 13))
                if front:
                    power(rstd3, var3, S["var3_ready"], b + 1, S["rstd3_ready"])
                if back:
                    scatter(b - 1, 1 - par, range(13, NT * K))

            norm1(0)
            pipeline(pool, step)

            def put(j, r):
                wait_apart(pool, S["y_done"], j + 1, S["pool_const"])
                for i in range(HB):
                    pool.indirect_dma_start(
                        result_rows, bass.IndirectOffsetOnAxis(ap=meta[r][:, i, 0:1].bitcast(I32), axis=0),
                        ye[r][:, i, :], None).then_inc(y_scattered[r], 16)

            with pool.Fori(0, TILES - BODY + 1, BODY) as j:
                for r in range(BODY):
                    put(j + r, r)

        @block.tensor
        def _(pe):
            pe.wait_ge(S["ident_ready"], 5)
            pe.wait_ge(S["attn_w_loaded"], 16 * 5)
            pe.transpose(bank[0][:, 0:P], wraw[:, 0, :], ident[:])
            pe.transpose(bank[0][:, P:2 * P], wraw[:, 2, :], ident[:])
            pe.transpose(bank[0][:, 2 * P:3 * P], wraw[:, 3, :], ident[:])
            pe.transpose(bank[0][:, 3 * P:4 * P], wraw[:, 4, :], ident[:])
            pe.matmul(bank[1][:, 0:P], wraw[:, 1, :], head_ones[:], start=True, stop=True)\
                .then_inc(S["setup_psum"], 1)
            pe.wait_ge(S["mod_w_loaded"], 32)
            pe.wait_ge(S["csilu_ready"], 1)
            pe.transpose(bank[2][:, 0:NB], csilu[:], ident[0:NB, 0:NB]).then_inc(S["setup_psum"], 1)
            pe.wait_ge(S["setup_copied"], 2)
            half = 3 * D
            pe.matmul(bank[3][0:NB, 0:half], csiluT[:], wmod_sb[:, 0:half], start=True, stop=True)
            pe.matmul(bank[4][0:NB, 0:half], csiluT[:], wmod_sb[:, half:2 * half], start=True, stop=True)
            pe.matmul(bank[5][:, 0:NB], wmod_sb[:, 0:D], csiluT[:], start=True, stop=True)
            pe.matmul(bank[5][:, NB:2 * NB], wmod_sb[:, D:2 * D], csiluT[:], start=True, stop=True)\
                .then_inc(S["setup_psum"], 1)
            pe.wait_ge(S["ffn_w_loaded"], 16 * 5)
            for m in range(M):
                pe.transpose(bank[6][:, m * P:(m + 1) * P], sgraw[:, m, :], ident[:])
                pe.transpose(bank[6][:, (M + m) * P:(M + m + 1) * P], suraw[:, m, :], ident[:])
                pe.transpose(bank[7][:, m * P:(m + 1) * P], sdraw[:, m * P:(m + 1) * P], ident[:])
            pe.transpose(bank[7][:, M * P:M * P + E], rraw[:], ident[0:E, 0:E]).then_inc(S["setup_psum"], 1)
            pe.wait_ge(S["setup_copied"], 4)

            def step(b, par, early, front, middle, back):
                f, g, h = b + 1, b, b - 1

                def pair(q):
                    n, m = q // M, q % M
                    src = h2T[1 - par][:, n * CH:(n + 1) * CH]
                    need(pe, S["silu_ready"], 4 * h + q)
                    pe.matmul(b_gate[:], SgT[:, m * P:(m + 1) * P], src, start=True, stop=True).then_inc(S["gate_ready"], 1)
                    need(pe, S["gu_ready"], 4 * h + q)
                    pe.matmul(b_up[:], SuT[:, m * P:(m + 1) * P], src, start=True, stop=True).then_inc(S["up_ready"], 1)

                def wo(n):
                    if n == 0:
                        pe.wait_ge(S["wo_scaled"], g + 1)
                    for t in range(TC):
                        at = (n * TC + t) * P
                        last = pe.matmul(b_O[n][:, t * P:(t + 1) * P], outT[:, at:at + P], Wo_b[:], start=True, stop=True)
                    last.then_inc(S["wo_ready"], 1)

                def turn_x(n):
                    if n == 0:
                        pe.wait_ge(S["xn1_ready"], f + 1)
                    else:
                        pe.wait_ge(S["h1T_ready"], NC * f + n)
                    for t in range(TC):
                        last = pe.transpose(b_T[:, t * P:(t + 1) * P], xn1[:, n * TC + t, :], ident[:])
                    last.then_inc(S["xT_ready"], 1)

                def project(n):
                    at = slice(n * CH, (n + 1) * CH)
                    if n == 0:
                        pe.wait_ge(S["h1T_ready"], NC * f + 1)
                    else:
                        pe.wait_ge(S["ks_done"], NC * f + n)
                    pe.matmul(b_proj[0][:], WrT[:], h1T[:, at], start=True, stop=True).then_inc(S["r_ready"], 1)
                    need(pe, S["kv_done"], NC * f + n)
                    pe.matmul(b_proj[1][:], WwT[:], h1T[:, at], start=True, stop=True).then_inc(S["w_ready"], 1)
                    pe.wait_ge(S["r_done"], NC * f + n + 1)
                    pe.matmul(b_proj[0][:], WksT[:], h1T[:, at], start=True, stop=True).then_inc(S["ks_ready"], 1)
                    pe.wait_ge(S["w_done"], NC * f + n + 1)
                    pe.matmul(b_proj[1][:], WvT[:], h1T[:, at], start=True, stop=True).then_inc(S["v_ready"], 1)

                def turn_h2(n):
                    if n == 0:
                        pe.wait_ge(S["h2_ready"], NC * g + 1)
                    else:
                        pe.wait_ge(S["h2T_ready"], NC * g + n)
                    for t in range(TC):
                        last = pe.transpose(b_T[:, t * P:(t + 1) * P], rows[par][:, n * TC + t, 0, 0:D], ident[:])
                    last.then_inc(S["h2xT_ready"], 1)

                def down(n):
                    if n == 0:
                        pe.wait_ge(S["sd_scaled"], h + 1)
                    for t in range(TC):
                        at = (n * TC + t) * P
                        if n == 0 and t == TC - 1 and middle:
                            pe.wait_ge(S["h2_ready"], NC * (g + 1))
                        for m in range(M):
                            last = pe.matmul(b_O[n][:, t * P:(t + 1) * P], guT[:, m, at:at + P], Sd_b[:, m, :],
                                             start=(m == 0), stop=(m == M - 1))
                    last.then_inc(S["down_ready"], 1)

                def logits_of(n):
                    pe.wait_ge(S["h2T_ready"], NC * g + n + 1)
                    for t in range(n * TC, (n + 1) * TC):
                        last = pe.matmul(b_small[:, LG + t * E:LG + (t + 1) * E], h2T[par][:, t * P:(t + 1) * P],
                                         RwT[:], start=True, stop=True)
                    return last

                def squares(n):
                    pe.wait_ge(S["sq_ready"], NC * f + n + 1)
                    for t in range(n * TC, (n + 1) * TC):
                        last = pe.matmul(b_small[:, SS + t:SS + t + 1], sqT[:, t * P:(t + 1) * P], ones_col[:, 0:1],
                                         start=True, stop=True)
                    return last

                if back:
                    pair(0)
                if middle:
                    wo(0)
                    wo(1)
                if back:
                    pair(1)
                    pe.wait_ge(S["picks_ready"], h + 1)
                    pe.matmul(b_small[:, PO:PO + E * NT], before[:], picks[:], start=True, stop=False)
                    pe.matmul(b_small[:, PO:PO + E * NT], ones_bf[:], picks_before[:], start=False, stop=True)
                    pe.matmul(b_small[:, CN:CN + E], ones_bf[:], picks_sum[:, NT - 1:E * NT:NT], start=True, stop=True)\
                        .then_inc(S["pos_ready"], 1)
                if back:
                    pair(2)
                if front:
                    turn_x(0)
                if back:
                    pair(3)
                if front:
                    turn_x(1)
                    project(0)
                    project(1)
                if middle:
                    turn_h2(0)
                if front:
                    squares(0)
                if back:
                    down(0)
                elif middle:
                    pe.wait_ge(S["h2_ready"], NC * (g + 1))
                if middle:
                    turn_h2(1)
                    logits_of(0)
                if back:
                    down(1)
                if middle:
                    last = logits_of(1)
                if front:
                    last = squares(1)
                if middle or front:
                    last.then_inc(S["small_ready"], 1)

            pipeline(pe, step)

            def turn(j, r):
                pe.wait_ge(xt_loaded[r], landed(j, r, XR))
                for i in range(HB):
                    if i == HB - 1:
                        need(pe, S["wc_done"], j)
                    last = pe.transpose(e_x[r % 2][:, i * P:(i + 1) * P], xt[r][:, i, 0:D], ident[:])
                last.then_inc(S["xtT_ready"], 1)

            def gate_up(j, r):
                pe.wait_ge(S["xT_done"], j + 1)
                for banks, at, done in ((e_gate, 0, "e_gate_ready"), (e_up, I, "e_up_ready")):
                    for m in range(M):
                        if at and m == M - 1:
                            need(pe, S["y_done"], j - 2)
                        last = pe.matmul(banks[r % 2][:, m * TR:(m + 1) * TR],
                                         wc[r % 2][:, at + m * P:at + (m + 1) * P], xT[r % 2], start=True, stop=True)
                    last.then_inc(S[done], 1)

            def down(j, r, e):
                pe.wait_ge(S["gu_done"], j + 1)
                for i in range(HB):
                    for m in range(M):
                        last = pe.matmul(e_y[r % 2][:, i * D:(i + 1) * D], guTe[r % 2][:, m, i * P:(i + 1) * P],
                                         Wexp[:, bass.ds(e + (2 * I + m * D), D)], start=(m == 0), stop=(m == M - 1))
                last.then_inc(S["y_psum"], 1)

            def step_e(j, r, turns=True, gates=True):
                e = weights_of(j, mybir.EngineType.PE)
                if turns:
                    turn(j + 2, (r + 2) % BODY)
                elif gates:
                    pe.wait_ge(S["wc_done"], j + 2)
                if gates:
                    gate_up(j + 1, (r + 1) % BODY)
                down(j, r, e)

            pe.wait_ge(S["base_ready"], NB * NC)
            pe.wait_ge(S["h2T_ready"], NB * NC)
            pe.wait_ge(S["pos_done"], NB)
            pe.wait_ge(S["expert_w_loaded"], 16 * 3 * E)
            pe.wait_ge(S["table_ready"], 1)
            turn(0, 0)
            turn(1, 1)
            gate_up(0, 0)
            for j in range(BODY):
                step_e(j, j)
            with pe.Fori(BODY, TILES - BODY, BODY) as j:
                for q in range(BODY):
                    step_e(j + q, q)
            for j in range(TILES - BODY, TILES):
                step_e(j, j % BODY, turns=j + 2 < TILES, gates=j + 1 < TILES)

        @block.scalar
        def _(act):
            act.wait_ge(S["mod_w_loaded"], 32)
            act.activation(csilu[:], craw[:], ACT.Silu).then_inc(S["csilu_ready"], 1)

            def normalise(out_, src, shift, rstd, tiles):
                for t in tiles:
                    last = act.activation(out_[:, t, :], src(t), ACT.Identity, bias=shift[:, t:t + 1],
                                          scale=rstd[:, t:t + 1])
                return last

            def norm_x(b, par):
                act.wait_ge(S["norm1_ready"], b + 1)
                normalise(xn1, lambda t: xb[par][:, t, :], shift1, rstd1, range(NT)).then_inc(S["xn1_ready"], 1)

            def touch(function):
                act.activation(touched[:], ones_e[0:1, 0:1], function).then_inc(S["touched"], 1)

            def step(b, par, early, front, middle, back):
                f, g = b + 1, b

                def norm_x1(n):
                    act.wait_ge(S["norm2_ready"], g + 1)
                    normalise(xn2, lambda t: resid_tiles(g, t, 1), shift2, rstd2, range(n * TC, (n + 1) * TC))\
                        .then_inc(S["xn2_done"], 1)

                def square(n):
                    at = slice(n * CH, (n + 1) * CH)
                    act.wait_ge(S["out_ready"], NC * f + n + 1)
                    act.activation(sqT[:, at], outT[:, at], ACT.Square).then_inc(S["sq_ready"], 1)

                def silu(q):
                    act.wait_ge(S["gate_ready"], 4 * (b - 1) + q + 1)
                    act.activation(sg[:, q, :], b_gate[:], ACT.Silu).then_inc(S["silu_ready"], 1)

                def modulate(n):
                    act.wait_ge(S["xT_ready"], NC * f + n + 1)
                    act.activation(h1T[:, n * CH:(n + 1) * CH], b_T[:], ACT.Identity, bias=cur_col[:, 0:1],
                                   scale=cur_col[:, 1:2]).then_inc(S["h1T_ready"], 1)

                if back:
                    for q in range(3):
                        silu(q)
                if front:
                    act.wait_ge(S["col_ready"], f + 1)
                    modulate(0)
                if back:
                    silu(3)
                if front:
                    touch(ACT.Sigmoid)
                    modulate(1)
                for n in range(NC):
                    at = slice(n * CH, (n + 1) * CH)
                    if front:
                        act.wait_ge(S["r_ready"], NC * f + n + 1)
                        act.activation(rT[:, at], b_proj[0][:], ACT.Sigmoid).then_inc(S["r_done"], 1)
                        act.wait_ge(S["w_ready"], NC * f + n + 1)
                        act.activation(wsig[:, at], b_proj[1][:], ACT.Sigmoid).then_inc(S["w_done"], 1)
                        if n == NC - 1 and middle:
                            norm_x1(n)
                        act.wait_ge(S["ks_ready"], NC * f + n + 1)
                        act.activation(ksT[:, at], b_proj[0][:], ACT.Copy).then_inc(S["ks_done"], 1)
                        if n < NC - 1 and middle:
                            norm_x1(n)
                    elif middle:
                        norm_x1(n)
                if front:
                    square(0)
                if middle:
                    for n in range(NC):
                        at = slice(n * TC, (n + 1) * TC)
                        act.wait_ge(S["h2_ready"], NC * g + n + 1)
                        act.activation(rows[par][:, at, 1, 0:D], rows[par][:, at, 0, 0:D], ACT.Copy)\
                            .then_inc(S["rows2_ready"], 1)
                        act.wait_ge(S["h2xT_ready"], NC * g + n + 1)
                        act.activation(h2T[par][:, n * CH:(n + 1) * CH], b_T[:], ACT.Copy).then_inc(S["h2T_ready"], 1)
                if front:
                    square(1)
                if early:
                    norm_x(b + 2, par)
                if middle:
                    act.wait_ge(S["logits_ready"], g + 1)
                    act.activation(probs[:], logits[:], ACT.Sigmoid).then_inc(S["probs_ready"], 1)
                    touch(ACT.Silu)

            norm_x(0, 0)
            pipeline(act, step)

            def copy_x(j, r):
                act.wait_ge(S["xtT_ready"], j + 1)
                act.activation(xT[r % 2], e_x[r % 2][:, 0:TR], ACT.Copy).then_inc(S["xT_done"], 1)

            def silu(j, r):
                act.wait_ge(S["e_gate_ready"], j + 1)
                act.activation(sge[r % 2], e_gate[r % 2][:], ACT.Silu).then_inc(S["silu_done"], 1)

            def step_e(j, r, turns=True):
                silu(j, r)
                if turns:
                    copy_x(j + 2, (r + 2) % BODY)

            copy_x(0, 0)
            copy_x(1, 1)
            with act.Fori(0, TILES - BODY, BODY) as j:
                for q in range(BODY):
                    step_e(j + q, q)
            for j in range(TILES - BODY, TILES):
                step_e(j, j % BODY, turns=j + 2 < TILES)

        @block.vector
        def _(dve):
            dve.wait_ge(S["iota_done"], 6)
            dve.tensor_copy(expert_iota[:], iota_i[:, 0:E])
            dve.tensor_copy(region_rows[:], iota_i[:, E:2 * E])
            dve.tensor_copy(running[:], iota_i[:, E:2 * E])
            dve.tensor_copy(dest_next[:], iota_i[:, 2 * E:2 * E + NT * K].rearrange("p (t k) -> p t k", k=K))
            dve.wait_ge(S["pool_const"], 12)
            dve.tensor_copy(spare_rows[:, :, D:D + 1].bitcast(I32).rearrange("p t o -> p (t o)"),
                            iota_i[:, 64:64 + SPARE_TILES * HB]).then_inc(S["spare_ready"], 1)
            dve.tensor_copy(pad_rows[:].rearrange("p e n w -> p (e n) w")[:, :, D:D + 1].bitcast(I32).rearrange("p t o -> p (t o)"),
                            iota_i[:, 32:32 + E * HB])
            dve.tensor_copy(tile_iota[:], iota_i[0:1, 96:96 + TILES]).then_inc(S["dve_const"], 1)
            dve.wait_ge(S["dve_const"], 1)
            dve.wait_ge(S["setup_psum"], 1)
            for i, w in enumerate((WrT, WvT, WwT, WoT)):
                dve.tensor_copy(w[:], bank[0][:, i * P:(i + 1) * P])
            dve.tensor_copy(WksT[:], bank[1][:, 0:P]).then_inc(S["setup_copied"], 1)
            dve.wait_ge(S["setup_psum"], 2)
            dve.tensor_copy(csiluT[:], bank[2][:, 0:NB]).then_inc(S["setup_copied"], 1)
            dve.wait_ge(S["setup_psum"], 3)
            mod_f = mod_sb[:].rearrange("b m d -> b (m d)")
            dve.tensor_copy(mod_f[:, 0:3 * D], bank[3][0:NB, 0:3 * D])
            dve.tensor_copy(mod_f[:, 3 * D:6 * D], bank[4][0:NB, 0:3 * D])
            dve.tensor_copy(mod_col[:, 0:2 * NB:2], bank[5][:, 0:NB])
            dve.tensor_scalar(mod_col[:, 1:2 * NB:2], bank[5][:, NB:2 * NB], 1.0, None, ALU.add)\
                .then_inc(S["setup_copied"], 1)
            dve.wait_ge(S["setup_copied"], 3)
            gates = mod_sb[:, 2:6:3, :]
            dve.tensor_scalar(sign_sb[:], gates, 0.0, 2.0, ALU.is_ge, ALU.mult)
            dve.scalar_tensor_tensor(out=mag_sb[:], in0=gates, scalar=-1.0, in1=gates, op0=ALU.mult, op1=ALU.max)\
                .then_inc(S["mod_step"], 1)
            dve.wait_ge(S["mod_step"], 1)
            dve.tensor_scalar(mag_sb[:], mag_sb[:], 0.25, None, ALU.max).then_inc(S["mod_step"], 1)
            dve.wait_ge(S["mod_step"], 2)
            dve.scalar_tensor_tensor(out=gates, in0=sign_sb[:], scalar=-1.0, in1=mag_sb[:], op0=ALU.add, op1=ALU.mult)
            dve.tensor_scalar(mod_sb[:, 4, :], mod_sb[:, 4, :], 1.0, None, ALU.add).then_inc(S["mod_ready"], 1)
            dve.wait_ge(S["setup_psum"], 4)
            dve.tensor_copy(SgT[:], bank[6][:, 0:I])
            dve.tensor_copy(SuT[:], bank[6][:, I:2 * I])
            dve.tensor_copy(SdT[:].rearrange("p m h -> p (m h)"), bank[7][:, 0:M * P])
            dve.tensor_copy(RwT[:], bank[7][:, M * P:M * P + E]).then_inc(S["setup_copied"], 1)
            dve.wait_ge(S["setup_copied"], 4)

            def scattered(b, par):
                batch = 16 * K * NT
                return (batch // 2) * b - (batch // 2) * par

            def stats_of(src, stats, s_stats):
                for t in range(NT):
                    last = dve.bn_stats(stats[:, t, :], src(t))
                last.then_inc(s_stats, 1)

            def norm_of(stats, mv, var, nmean, count, s_stats, s_mv, s_var, free=None):
                wait_apart(dve, s_stats, count, S["dve_const"])
                for t in range(NT):
                    last = dve.bn_aggr(mv[:, t, :], stats[:, t, :])
                last.then_inc(s_mv, 1)
                if free:
                    free()
                dve.wait_ge(s_mv, count)
                dve.tensor_scalar(var[:], mv[:, :, 1], LN_EPS, None, ALU.add)
                dve.tensor_scalar(nmean[:], mv[:, :, 0], -1.0, None, ALU.mult).then_inc(s_var, 1)

            def stats_x(b, par):
                wait_apart(dve, x_loaded[par], landed(b, par, 2), S["dve_const"])
                stats_of(lambda t: xb[par][:, t, :], stats1, S["stats1_done"])

            def norm_x(b):
                norm_of(stats1, mv1, var1, nmean1, b + 1, S["stats1_done"], S["mv1_done"], S["var1_ready"],
                        lambda: need(dve, S["xn1_ready"], b))

            def columns(b):
                dve.tensor_copy(cur_col[:], mod_col[:, bass.ds(b * 2, 2)]).then_inc(S["col_ready"], 1)

            def step(b, par, early, front, middle, back):
                f, g, h = b + 1, b, b - 1

                def mult(q):
                    n, m = q // M, q % M
                    dve.wait_ge(S["up_ready"], 4 * h + q + 1)
                    dve.wait_ge(S["silu_ready"], 4 * h + q + 1)
                    if q == 0:
                        need(dve, S["down_ready"], NC * h)
                    dve.tensor_tensor(guT[:, m, n * CH:(n + 1) * CH], sg[:, q, :], b_up[:], ALU.mult)\
                        .then_inc(S["gu_ready"], 1)

                def add_x(n):
                    if n == 0:
                        dve.wait_ge(S["rstd3_ready"], g + 1)
                    dve.wait_ge(S["wo_ready"], NC * g + n + 1)
                    for t in range(n * TC, (n + 1) * TC):
                        last = dve.scalar_tensor_tensor(
                            out=resid_tiles(g, t, 1), in0=b_O[n][:, (t % TC) * P:(t % TC + 1) * P],
                            scalar=rstd3[:, t:t + 1], in1=xb[par][:, t, :], op0=ALU.mult, op1=ALU.add)
                    if n == NC - 1:
                        last.then_inc(S["x1_ready"], 1)

                def decay_kv(n):
                    at = slice(n * CH, (n + 1) * CH)
                    dve.wait_ge(S["w_done"], NC * f + n + 1)
                    dve.tensor_scalar(wsig[:, at], wsig[:, at], 0.99, None, ALU.mult)
                    dve.wait_ge(S["ks_done"], NC * f + n + 1)
                    dve.wait_ge(S["v_ready"], NC * f + n + 1)
                    dve.tensor_tensor(ksT[:, at], ksT[:, at], b_proj[1][:], ALU.mult).then_inc(S["kv_done"], 1)

                def recur(n):
                    at = slice(n * CH, (n + 1) * CH)
                    dve.wait_ge(S["kv_done"], NC * f + n + 1)
                    dve.tensor_tensor_scan(stateT[:, at], wsig[:, at], ksT[:, at],
                                           0.0 if n == 0 else stateT[:, n * CH - 1:n * CH], ALU.mult, ALU.add)\
                        .then_inc(S["state_done"], 1)
                    dve.wait_ge(S["state_done"], NC * f + n + 1)
                    dve.tensor_tensor(outT[:, at], stateT[:, at], rT[:, at], ALU.mult).then_inc(S["out_ready"], 1)

                if back:
                    mult(0)
                if middle:
                    add_x(0)
                if back:
                    mult(1)
                    dve.wait_ge(S["pos_ready"], h + 1)
                    ev = lambda a: a.rearrange("p (e t) -> p e t", e=E)
                    dve.tensor_tensor(ev(pos[:]), ev(b_small[:, PO:PO + E * NT]),
                                      running[:].unsqueeze(2).to_broadcast([P, E, NT]), ALU.add)
                    dve.tensor_tensor(tmpf[:], running[:], b_small[:, CN:CN + E], ALU.add).then_inc(S["pos_done"], 1)
                    dve.wait_ge(S["pos_done"], h + 1)
                    dve.tensor_copy(running[:], tmpf[:])
                    pv = pos[:].rearrange("p (e t) -> p t e", e=E)
                    for k in range(K):
                        last = dve.tensor_tensor(prod[:, k], onehot[:, k], pv, ALU.mult)
                    last.then_inc(S["prod_done"], 1)
                    dve.wait_ge(S["prod_done"], h + 1)
                    dve.tensor_reduce(slotf[:], prod[:].rearrange("p k t e -> p (k t) e"), AX_X, ALU.add)\
                        .then_inc(S["slotf_done"], 1)
                    dve.wait_ge(S["slotf_done"], h + 1)
                    need(dve, rows_scattered[par], scattered(b, par))
                    dve.tensor_copy(slots[:], slotf[:]).then_inc(S["slots_ready"], 1)
                if middle:
                    add_x(1)
                if back:
                    mult(2)
                if middle:
                    wait_apart(dve, S["x1_ready"], g + 1, S["dve_const"])
                    stats_of(lambda t: resid_tiles(g, t, 1), stats2, S["stats2_done"])
                    norm_of(stats2, mv2, var2, nmean2, g + 1, S["stats2_done"], S["mv2_done"], S["var2_ready"])
                if back:
                    mult(3)
                    dve.wait_ge(S["mod_row_loaded"], 16)
                    need(dve, S["down_ready"], NC * h)
                    for m in range(M):
                        last = dve.tensor_tensor(Sd_b[:, m, :], SdT[:, m, :], mod_at(h, 3), ALU.mult)
                    last.then_inc(S["sd_scaled"], 1)
                if early:
                    stats_x(b + 2, par)
                if front:
                    decay_kv(0)
                if early:
                    norm_x(b + 2)
                if front:
                    recur(0)
                if middle:
                    over = lambda a: a.unsqueeze(1).to_broadcast([P, TC, D])
                    for n in range(NC):
                        at = slice(n * TC, (n + 1) * TC)
                        dve.wait_ge(S["xn2_done"], NC * g + n + 1)
                        dve.tensor_tensor(xn2[:, at], xn2[:, at], over(mod_at(g, 2)), ALU.mult).then_inc(S["h2_scaled"], 1)
                        dve.wait_ge(S["h2_scaled"], NC * g + n + 1)
                        dve.tensor_tensor(rows[par][:, at, 0, 0:D], xn2[:, at], over(mod_at(g, 1)), ALU.add)\
                            .then_inc(S["h2_ready"], 1)
                if front:
                    decay_kv(1)
                    recur(1)
                if early:
                    columns(b + 2)
                if back:
                    for n in range(NC):
                        dve.wait_ge(S["down_ready"], NC * h + n + 1)
                        tiles = resid_tiles(h, n * TC, TC)
                        dve.tensor_tensor(tiles, b_O[n][:], tiles, ALU.add).then_inc(S["base_ready"], 1)
                if front:
                    dve.wait_ge(S["mod_row_loaded"], 16)
                    dve.tensor_tensor(Wo_b[:], WoT[:], mod_at(f, 0), ALU.mult).then_inc(S["wo_scaled"], 1)
                if front or middle:
                    dve.wait_ge(S["small_ready"], b + 2)
                if front:
                    dve.tensor_scalar(var3[:], b_small[:, SS:SS + NT], 1.0 / D, RMS_EPS, ALU.mult, ALU.add)\
                        .then_inc(S["var3_ready"], 1)
                if middle:
                    dve.tensor_tensor(logits[:], b_small[:, LG:LG + NT * E].rearrange("p (t e) -> p t e", e=E),
                                      bias_row[:].unsqueeze(1).to_broadcast([P, NT, E]), ALU.add)\
                        .then_inc(S["logits_ready"], 1)
                    wait_apart(dve, S["probs_ready"], g + 1, S["dve_const"])
                    for t in range(NT):
                        last = dve.max(top[:, t, :], probs[:, t, :])
                    last.then_inc(S["top_done"], 1)
                    wait_apart(dve, S["top_done"], g + 1, S["dve_const"])
                    for t in range(NT):
                        last = dve.max_index(topi[:, t, :], top[:, t, :], probs[:, t, :])
                    last.then_inc(S["topi_done"], 1)
                    dve.tensor_tensor(den[:], top[:, :, 0], top[:, :, 1], ALU.add).then_inc(S["den_done"], 1)
                    dve.wait_ge(S["topi_done"], g + 1)
                    dve.tensor_copy(topf[:], topi[:, :, 0:K].rearrange("p t k -> p k t")).then_inc(S["topf_done"], 1)
                    dve.wait_ge(S["den_done"], g + 1)
                    dve.reciprocal(rden[:], den[:]).then_inc(S["rden_done"], 1)
                    dve.wait_ge(S["topf_done"], g + 1)
                    for k in range(K):
                        last = dve.tensor_tensor(onehot[:, k], topf[:, k, :].unsqueeze(2).to_broadcast([P, NT, E]),
                                                 expert_iota[:].unsqueeze(1).to_broadcast([P, NT, E]), ALU.is_equal)
                    last.then_inc(S["onehot_done"], 1)
                    dve.wait_ge(S["rden_done"], g + 1)
                    dve.tensor_tensor(rows[par][:, :, :, D + 1], top[:, :, 0:K],
                                      rden[:].unsqueeze(2).to_broadcast([P, NT, K]), ALU.mult)
                    dve.tensor_copy(rows[par][:, :, :, D].bitcast(I32), dest_next[:]).then_inc(S["meta_ready"], 1)
                    dve.wait_ge(S["onehot_done"], g + 1)
                    dve.tensor_tensor(picks[:].rearrange("p (e t) -> p t e", e=E), onehot[:, 0], onehot[:, 1], ALU.add)\
                        .then_inc(S["picks_done"], 1)
                    dve.wait_ge(S["picks_done"], g + 1)
                    dve.tensor_tensor_scan(picks_sum[:], tile_start[:], picks[:], 0.0, ALU.mult, ALU.add)\
                        .then_inc(S["picks_sum_done"], 1)
                    dve.wait_ge(S["picks_sum_done"], g + 1)
                    dve.tensor_tensor(picks_before[:], picks_sum[:], picks[:], ALU.subtract).then_inc(S["picks_ready"], 1)
                    dve.wait_ge(S["meta_ready"], g + 1)
                    dve.tensor_scalar(dest_next[:], dest_next[:], float(K * T), None, ALU.add)

            stats_x(0, 0)
            norm_x(0)
            columns(0)
            pipeline(dve, step)

            count = [0]

            def then(instruction):
                count[0] += 1
                instruction.then_inc(S["table_step"], 1)
                dve.wait_ge(S["table_step"], count[0])

            dve.tensor_copy(tab[:, 2 * TILES:2 * TILES + E], tmpf[0:1, :]).then_inc(S["ends_ready"], 1)
            then(dve.tensor_tensor(counts[:], tmpf[:], region_rows[:], ALU.subtract))
            then(dve.tensor_scalar(tmpi[:], counts[:], float(TR - 1), None, ALU.add))
            then(dve.tensor_scalar(tilesi[:], tmpi[:], TR.bit_length() - 1, None, ALU.arith_shift_right))
            then(dve.tensor_copy(tilesf[:], tilesi[:]))
            then(dve.tensor_tensor_scan(ends[:], ones_e[:], tilesf[:], 0.0, ALU.mult, ALU.add))
            then(dve.tensor_scalar(skip[:], tilesf[:], -1.0, float(REGION // TR), ALU.mult, ALU.add))
            over_e = lambda a: a.unsqueeze(1).to_broadcast([1, TILES, E])
            then(dve.tensor_tensor(passed[:], tile_iota[:].unsqueeze(2).to_broadcast([1, TILES, E]),
                                   over_e(ends[0:1, :]), ALU.is_ge))
            then(dve.tensor_tensor(passed_skip[:], passed[:], over_e(skip[0:1, :]), ALU.mult))
            dve.tensor_reduce(tab_f[:, 0, :], passed[:], AX_X, ALU.add)
            then(dve.tensor_reduce(tab_f[:, 1, :], passed_skip[:], AX_X, ALU.add))
            then(dve.tensor_tensor(tab_g[:, 1, :], tab_f[:, 1, :], tile_iota[:], ALU.add))
            dve.tensor_scalar(tab[:, TILES:2 * TILES], tab_g[:, 1, :], float(TR), None, ALU.mult)
            dve.tensor_scalar(tab[:, 0:TILES], tab_f[:, 0, :], float(E - 1), float(WE), ALU.min, ALU.mult).then_inc(S["table_ready"], 1)

            def mult_e(j, r):
                dve.wait_ge(S["e_up_ready"], j + 1)
                dve.wait_ge(S["silu_done"], j + 1)
                dve.tensor_tensor(guTe[r % 2].rearrange("p m t -> p (m t)"), sge[r % 2], e_up[r % 2][:], ALU.mult)\
                    .then_inc(S["gu_done"], 1)

            def copy_w(j, r, e):
                dve.tensor_copy(wc[r % 2], Wexp[:, bass.ds(e, 2 * I)]).then_inc(S["wc_done"], 1)

            def copy_meta(j, r):
                dve.wait_ge(xt_loaded[r], landed(j, r, XR))
                need(dve, y_scattered[r], (16 * HB // XR) * j - (16 * HB // XR) * r)
                dve.tensor_copy(meta[r][:], xt[r][:, :, D:D + 2]).then_inc(S["meta_done"], 1)

            def scale_y(j, r):
                dve.wait_ge(S["meta_done"], j + 1)
                dve.wait_ge(S["y_psum"], j + 1)
                for i in range(HB):
                    last = dve.tensor_scalar(ye[r][:, i, :], e_y[r % 2][:, i * D:(i + 1) * D], meta[r][:, i, 1:2], None,
                                             ALU.mult)
                last.then_inc(S["y_done"], 1)

            def step_e(j, r, copies=True, scales=True):
                if copies:
                    e = weights_of(j + 2, mybir.EngineType.DVE)
                mult_e(j, r)
                if copies:
                    copy_w(j + 2, (r + 2) % BODY, e)
                copy_meta(j, r)
                if scales:
                    scale_y(j - 1, (r - 1) % BODY)

            dve.wait_ge(S["expert_w_loaded"], 16 * 3 * E)
            dve.wait_ge(S["table_ready"], 1)
            for j in range(2):
                copy_w(j, j, weights_of(j, mybir.EngineType.DVE))
            for j in range(BODY):
                step_e(j, j, scales=j > 0)
            with dve.Fori(BODY, TILES - BODY, BODY) as j:
                for q in range(BODY):
                    step_e(j + q, q)
            for j in range(TILES - BODY, TILES):
                step_e(j, j % BODY, copies=j + 2 < TILES)
            scale_y(TILES - 1, (TILES - 1) % BODY)

            def combine(b, n, r, i):
                dve.wait_ge(yb_loaded[r], 16 * (b + 1))
                dve.tensor_tensor(acc[r], yb[r][:, :, 0, :], yb[r][:, :, 1, :], ALU.add).then_inc(S["y_sum"], 1)
                dve.wait_ge(S["y_sum"], i + 1)
                dve.tensor_tensor(acc[r], acc[r], mod_at(b, 3).unsqueeze(1).to_broadcast([P, TC, D]), ALU.mult)\
                    .then_inc(S["y_gated"], 1)
                dve.wait_ge(S["y_gated"], i + 1)
                need(dve, out_stored[r], 16 * b)
                dve.tensor_tensor(fin[r].rearrange("p t d -> p (t d)"), acc[r].rearrange("p t d -> p (t d)"),
                                  resid_tiles(b, n * TC, TC), ALU.add).then_inc(S["fin_ready"], 1)

            for n in range(NC):
                combine(0, n, n, n)
            with dve.Fori(1, NB) as b:
                for n in range(NC):
                    combine(b, n, n, b * NC + n)


_INS = ["L0_attn_x", "L0_attn_Wr", "L0_attn_Wk", "L0_attn_Wv", "L0_attn_Ww", "L0_attn_Wo", "L0_ffn_shared_gate",
        "L0_ffn_shared_up", "L0_ffn_shared_down", "L0_ffn_gate_w", "L0_ffn_up_w", "L0_ffn_down_w",
        "L0_ffn_router_w", "L0_ffn_routing_bias", "L0_c", "L0_wmod"]


def kernel(**inputs):
    import numpy as np
    import concourse.bacc as bacc
    from concourse.bass_utils import run_bass_kernel_spmd

    nc = bacc.Bacc("TRN2", target_bir_lowering=False, num_devices=1)
    arrays, args = {}, []
    for name in _INS:
        a = np.ascontiguousarray(inputs[name])
        arrays[f"in_{name}"] = a
        args.append(nc.dram_tensor(f"in_{name}", a.shape, mybir.dt.from_np(a.dtype), kind="ExternalInput").ap())
    out = nc.dram_tensor("out_0", inputs["L0_attn_x"].shape, F32, kind="ExternalOutput").ap()
    build(nc, *args, out)
    r = run_bass_kernel_spmd(nc, [arrays], core_ids=[0])
    return r.results[0]["out_0"]
```

```python
from contextlib import ExitStack

import concourse.bass as bass
from concourse import mybir

ALU = mybir.AluOpType
ACT = mybir.ActivationFunctionType
F32 = mybir.dt.float32
F32R = mybir.dt.float32r
BF16 = mybir.dt.bfloat16
I32 = mybir.dt.int32
U32 = mybir.dt.uint32
AX_X = mybir.AxisListType.X

P = 128


def need(engine, semaphore, count):
    if isinstance(count, int) and count <= 0:
        return
    engine.wait_ge(semaphore, count)


def wait_apart(engine, semaphore, count, met):
    if isinstance(count, int):
        engine.wait_ge(semaphore, count)
        return
    count = engine.to_reg(count)
    engine.wait_ge(met, 1)
    engine.wait_ge(semaphore, count)


def landed(k, slot, ring, each=16):
    return (each // ring) * k + (each - (each // ring) * slot)


def build(nc, x, Wr, Wk, Wv, Ww, Wo, shared_gate, shared_up, shared_down, gate_w, up_w, down_w,
          router_w, routing_bias, c, wmod, out):
    NB, T, D = x.shape
    NH = 16
    HD = D // NH
    E, _, I = gate_w.shape
    M = I // P
    K = 2
    NT = T // P
    CH = 512
    NC = T // CH
    TC = CH // P
    TOKENS = NB * T
    TR = 2 * P
    HB = TR // P
    REGION = TOKENS + TR
    BODY = 4
    TILES = TOKENS * K // TR + E - 1
    LOOPED = (TILES - 2) // BODY * BODY
    SPARE_TILES = TILES - TOKENS * K // TR
    SPARE0 = E * REGION
    ROWS = SPARE0 + SPARE_TILES * TR
    W = 132
    YPAD0 = TOKENS * K
    YROWS = YPAD0 + (E + SPARE_TILES) * TR
    LN_EPS = 1e-5
    RMS_EPS = 1.1920928955078125e-07

    with ExitStack() as ctx:
        def sb(name, shape, dt=F32):
            return ctx.enter_context(nc.sbuf_tensor(name, shape, dt))

        def sem(name):
            return ctx.enter_context(nc.semaphore(name))

        bank = [ctx.enter_context(nc.psum_tensor(f"bank{i}", [P, 512], F32)) for i in range(8)]

        expert_rows = nc.dram_tensor("expert_rows", (ROWS, W), F32).ap()
        result_rows = nc.dram_tensor("result_rows", (YROWS, D), F32).ap()
        mod_rows = nc.dram_tensor("mod_rows", (NB, 2 * D), F32).ap()

        ident = sb("ident", [P, P])
        head_ones = sb("head_ones", [P, P])
        before = sb("before", [P, P], BF16)
        ones_bf = sb("ones_bf", [P, P], BF16)
        ones_col = sb("ones_col", [P, 2])
        minus_half = sb("minus_half", [P, NT])
        tile_start = sb("tile_start", [P, E * NT])
        iota_i = sb("iota_i", [P, 256], I32)
        expert_iota = sb("expert_iota", [P, E])
        region_rows = sb("region_rows", [P, E])
        running = sb("running", [P, E])
        dest_next = sb("dest_next", [P, NT, K])
        rraw = sb("rraw", [E, P])
        craw = sb("craw", [NB, D])
        bias_row = sb("bias_row", [P, E])
        WoT = sb("WoT", [P, P])
        SPLIT_CHUNK = 1
        WaT = sb("WaT", [P, 4 * P])
        Wa_hi = sb("Wa_hi", [P, 4 * P], F32R)
        Wa_lo = sb("Wa_lo", [P, 4 * P], F32R)
        Wo_b = sb("Wo_b", [P, P])
        Sgu_hi = sb("Sgu_hi", [P, 2 * I], F32R)
        Sgu_lo = sb("Sgu_lo", [P, 2 * I], F32R)
        SdT = sb("SdT", [P, M, P])
        Sd_b = sb("Sd_b", [P, M, P])
        RwT = sb("RwT", [P, E])
        WE = 2 * I + M * D
        Wexp = sb("Wexp", [P, E * WE])

        csilu = sb("csilu", [NB, D])
        csiluT = sb("csiluT", [P, NB])
        mod_sb = sb("mod_sb", [NB, 6, D])
        sign_sb = sb("sign_sb", [NB, 2, D])
        mag_sb = sb("mag_sb", [NB, 2, D])
        COLS = 4
        mod_col = sb("mod_col", [P, NB * COLS])
        cur_col = sb("cur_col", [P, 2])
        cur_col2 = sb("cur_col2", [P, 2])
        mod_row = sb("mod_row", [P, NB * 2 * D])

        xb = [sb(f"xb{i}", [P, NT, D]) for i in range(2)]
        stats1 = sb("stats1", [P, NT, 6])
        mv1 = sb("mv1", [P, NT, 2])
        var1 = sb("var1", [P, NT])
        rstd1 = sb("rstd1", [P, NT])
        nmean1 = sb("nmean1", [P, NT])
        shift1 = sb("shift1", [P, NT])
        xn1 = sb("xn1", [P, NT, D])
        h1T = sb("h1T", [P, T])
        h1_hi = sb("h1_hi", [P, CH], F32R)
        h1_lo = sb("h1_lo", [P, CH], F32R)
        rT = sb("rT", [P, T])
        wsig = sb("wsig", [P, T])
        ksT = sb("ksT", [P, T])
        stateT = sb("stateT", [P, T])
        outT = sb("outT", [P, T])
        sqT = sb("sqT", [P, T])
        wraw = sqT[:, 0:5 * P].rearrange("p (i n) -> p i n", i=5)
        sgraw = outT[:, 0:I].rearrange("p (m n) -> p m n", m=M)
        suraw = outT[:, I:2 * I].rearrange("p (m n) -> p m n", m=M)
        sdraw = outT[:, 2 * I:3 * I]
        wmod_sb = stateT[:, 0:6 * D]
        resid = sb("resid", [P, NB * NT * D])
        var3 = sb("var3", [P, NT])
        rstd3 = sb("rstd3", [P, NT])
        stats2 = sb("stats2", [P, NT, 6])
        mv2 = sb("mv2", [P, NT, 2])
        var2 = sb("var2", [P, NT])
        rstd2 = sb("rstd2", [P, NT])
        nmean2 = sb("nmean2", [P, NT])
        shift2 = sb("shift2", [P, NT])
        xn2 = sb("xn2", [P, NT, D])
        rows = [sb(f"rows{i}", [P, NT, K, W]) for i in range(2)]
        h2T = sb("h2T", [P, T])
        h2_hi = sb("h2_hi", [P, T], F32R)
        h2_lo = sb("h2_lo", [P, T], F32R)
        logits = sb("logits", [P, NT, E])
        probs = sb("probs", [P, NT, E])
        top = sb("top", [P, NT, 8])
        topi = sb("topi", [P, NT, 8], U32)
        topf = sb("topf", [P, K, NT])
        onehot = sb("onehot", [P, K, NT, E])
        picks = sb("picks", [P, E * NT], BF16)
        picks_sum = sb("picks_sum", [P, E * NT], BF16)
        picks_before = sb("picks_before", [P, E * NT], BF16)
        den = sb("den", [P, NT])
        rden = sb("rden", [P, NT])
        pos = sb("pos", [P, E * NT])
        prod = sb("prod", [P, K, NT, E])
        slotf = sb("slotf", [P, K * NT])
        slots = sb("slots", [P, K * NT], I32)
        sg = sb("sg", [P, 4, CH])
        guT = sb("guT", [P, M, T])
        counts = sb("counts", [P, E])
        tmpf = sb("tmpf", [P, E])
        tmpi = sb("tmpi", [P, E], I32)
        tilesi = sb("tilesi", [P, E], I32)
        tilesf = sb("tilesf", [P, E])
        ends = sb("ends", [P, E])
        skip = sb("skip", [P, E])
        ones_e = sb("ones_e", [P, E])
        touched = sb("touched", [1, 1])
        pad_rows = sb("pad_rows", [P, E, HB, W])
        spare_rows = resid[:, 0:SPARE_TILES * HB * W].rearrange("p (n w) -> p n w", w=W)
        tile_iota = sb("tile_iota", [1, TILES])
        passed = stateT[0:1, 0:TILES * E].rearrange("a (j e) -> a j e", e=E)
        passed_skip = outT[0:1, 0:TILES * E].rearrange("a (j e) -> a j e", e=E)
        tab_f = sb("tab_f", [1, 2, TILES])
        tab_g = sb("tab_g", [1, 2, TILES])
        tab = sb("tab", [1, 2 * TILES + E], I32)
        XR = 4
        xt = [sb(f"xt{i}", [P, HB, W]) for i in range(XR)]
        meta = [sb(f"meta{i}", [P, HB, 2]) for i in range(XR)]
        x_hi = [sb(f"x_hi{i}", [P, TR], F32R) for i in range(2)]
        x_lo = [sb(f"x_lo{i}", [P, TR], F32R) for i in range(2)]
        halves = lambda a: [a[:, 0:CH], a[:, CH:2 * CH]]
        w_hi, w_lo = halves(h2_hi), halves(h2_lo)
        sge = halves(outT)
        guTe = [guT[:, 0, i * M * TR:(i + 1) * M * TR].rearrange("p (m t) -> p m t", m=M) for i in range(2)]
        ye = [stateT[:, i * TR:(i + 1) * TR].rearrange("p (n d) -> p n d", n=HB) for i in range(XR)]
        chunk = lambda a: a.rearrange("p (t d) -> p t d", d=D)
        flat_rows = [rows[i][:].rearrange("p t k w -> p (t k w)")[:, 0:CH * K] for i in range(2)]
        flat_xn = [a[:].rearrange("p t d -> p (t d)") for a in (xn1, xn2)]
        YR = 2 * NC
        yb = [a.rearrange("p (t k d) -> p t k d", k=K, d=D) for a in flat_rows + flat_xn]
        acc = [chunk(a[:, i * CH:(i + 1) * CH]) for a in (h1T, sqT) for i in range(NC)]
        fin = [chunk(a[:, i * CH:(i + 1) * CH]) for a in (rT, wsig) for i in range(NC)]

        S = {}
        for name in (
            "attn_w_loaded", "mod_w_loaded", "ffn_w_loaded", "expert_w_loaded", "mod_stored", "mod_row_loaded",
            "pool_const", "ident_ready", "iota_done", "dve_const", "setup_psum", "setup_copied", "csilu_ready", "mod_step",
            "mod_ready", "split_step",
            "stats1_done", "mv1_done", "var1_ready", "rstd1_ready", "norm1_ready", "col_ready", "xn1_ready",
            "xT_ready", "h1T_ready", "r_ready", "w_ready", "ks_ready", "v_ready", "r_done", "w_done", "ks_done",
            "kv_done", "state_done", "out_ready", "sq_ready",
            "small_ready", "var3_ready", "rstd3_ready", "wo_scaled", "wo_ready", "x1_ready", "stats2_done", "mv2_done",
            "var2_ready", "rstd2_ready", "norm2_ready", "xn2_done", "h1_hi_ready", "h1_lo_ready", "h2xT_ready", "h2_back", "h2_hi_ready", "h2_lo_ready", "h2T_ready",
            "rows_ready", "logits_ready", "probs_ready", "top_done", "topi_done", "topf_done", "onehot_done",
            "picks_done", "picks_sum_done", "picks_ready", "den_done", "rden_done", "meta_ready",
            "pos_ready", "pos_done", "prod_done", "slotf_done", "slots_ready", 
            "gate_ready", "up_ready", "silu_ready", "gu_ready", "sd_scaled", "down_ready", "base_ready", "touched",
            "table_step", "ends_ready", "table_ready", "spare_ready", "spare_stored", "pads_stored",
            "xtT_ready", "x_hi_done", "x_lo_done", "w_hi_done", "w_lo_done", "e_gate_ready", "e_up_ready", "silu_done", "meta_done", "gu_done",
            "y_psum", "y_done", 
            "y_sum", "y_gated", "fin_ready", 
        ):
            S[name] = sem(name)
        x_loaded = [sem(f"x_loaded{i}") for i in range(2)]
        rows_scattered = [sem(f"rows_scattered{i}") for i in range(2)]
        xt_loaded = [sem(f"xt_loaded{i}") for i in range(XR)]
        y_scattered = [sem(f"y_scattered{i}") for i in range(XR)]
        yb_loaded = [sem(f"yb_loaded{i}") for i in range(YR)]
        out_stored = [sem(f"out_stored{i}") for i in range(YR)]

        x_v = x.rearrange("b (t p) d -> p (b t) d", p=P)
        res_v = resid[:, :]
        out_v = out.rearrange("b (t p) d -> p (b t) d", p=P)
        y_v = result_rows[0:TOKENS * K, :].rearrange("(n p k) d -> p n k d", p=P, k=K)

        def mod_at(b, which):
            return mod_row[:, bass.ds((b * 2 + which) * D, D)]

        def resid_tiles(b, t, n):
            return res_v[:, bass.ds((b * NT + t) * D, n * D)]

        b_T, b_small = bank[0], bank[1]
        b_proj = [[bank[2], bank[3]], [bank[6], bank[7]]]
        b_O = [bank[4], bank[5]]
        b_gate, b_up = bank[6], bank[7]
        SS, LG, PO, CN = 0, 8, 8 + NT * E, 8 + 2 * NT * E

        e_x = [bank[0], bank[1]]
        e_gate, e_up = [bank[2], bank[3]], [bank[4], bank[5]]
        e_y = [bank[6], bank[7]]

        def weights_of(j, engine):
            return nc.values_load_multi_w_load_instructions(
                tab[0:1, bass.ds(j, 1)], engines=[engine], min_val=0, max_val=(E - 1) * WE,
                skip_runtime_bounds_check_because="the table's values are clamped")[1][0]

        block = ctx.enter_context(nc.Block())

        def pipeline(eng, step):
            step(-1, 1, True, True, False, False)
            step(0, 0, True, True, True, False)
            step(1, 1, True, True, True, True)
            with eng.Fori(2, NB - 3, 2) as b:
                step(b, 0, True, True, True, True)
                step(b + 1, 1, True, True, True, True)
            step(NB - 2, 0, False, True, True, True)
            step(NB - 1, 1, False, False, True, True)
            step(NB, 0, False, False, False, True)

        @block.sync
        def _(sp):
            sp.dma_start(xb[0][:], x_v[:, 0:NT, :]).then_inc(x_loaded[0], 16)
            sp.dma_start(craw[:], c).then_inc(S["mod_w_loaded"], 16)
            sp.dma_start(wmod_sb, wmod).then_inc(S["mod_w_loaded"], 16)
            for i, w in enumerate((Wr, Wk, Wv, Ww, Wo)):
                sp.dma_start(wraw[:, i, :], w).then_inc(S["attn_w_loaded"], 16)
            sp.dma_start(xb[1][:], x_v[:, NT:2 * NT, :]).then_inc(x_loaded[1], 16)
            sp.dma_start(sgraw, shared_gate.rearrange("(m p) h -> p m h", p=P)).then_inc(S["ffn_w_loaded"], 16)
            sp.dma_start(suraw, shared_up.rearrange("(m p) h -> p m h", p=P)).then_inc(S["ffn_w_loaded"], 16)
            sp.dma_start(sdraw, shared_down).then_inc(S["ffn_w_loaded"], 16)
            sp.dma_start(rraw[:], router_w).then_inc(S["ffn_w_loaded"], 16)
            sp.dma_start(bias_row[:], routing_bias.rearrange("(a e) -> a e", a=1).to_broadcast([P, E]))\
                .then_inc(S["ffn_w_loaded"], 16)
            sp.wait_ge(S["spare_ready"], 1)
            sp.dma_start(expert_rows[SPARE0:ROWS, :].rearrange("(n p) w -> p n w", p=P), spare_rows)\
                .then_inc(S["spare_stored"], 16)
            sp.wait_ge(S["mod_ready"], 1)
            sp.dma_start(mod_rows.rearrange("b (m d) -> b m d", d=D), mod_sb[:, 2:6:3, :]).then_inc(S["mod_stored"], 16)
            sp.wait_ge(S["mod_stored"], 16)
            sp.dma_start(mod_row[:], mod_rows.rearrange("b n -> (b n)").rearrange("(a n) -> a n", a=1)
                         .to_broadcast([P, NB * 2 * D])).then_inc(S["mod_row_loaded"], 16)
            for e in range(E):
                wg = Wexp[:, e * WE:(e + 1) * WE]
                sp.dma_start(wg[:, 0:I], gate_w[e]).then_inc(S["expert_w_loaded"], 16)
                sp.dma_start(wg[:, I:2 * I], up_w[e]).then_inc(S["expert_w_loaded"], 16)
                sp.dma_start(wg[:, 2 * I:WE].rearrange("p (m h) -> p m h", m=M),
                             down_w[e].rearrange("(m p) h -> p m h", p=P)).then_inc(S["expert_w_loaded"], 16)
            def load_x(b, par):
                sp.wait_ge(S["x1_ready"], b - 1)
                sp.dma_start(xb[par][:], x_v[:, bass.ds(b * NT, NT), :]).then_inc(x_loaded[par], 16)

            with sp.Fori(2, NB - 1, 2) as b:
                load_x(b, 0)
                load_x(b + 1, 1)

            def load_tile(j, r):
                first = sp.value_load(tab[0:1, bass.ds(TILES + j, 1)], min_val=0, max_val=SPARE0 + (SPARE_TILES - 1) * TR)
                need(sp, S["xtT_ready"], j - XR + 1)
                need(sp, S["meta_done"], j - XR + 1)
                sp.dma_start(xt[r][:], expert_rows[bass.ds(first, TR), :].rearrange("(p n) w -> p n w", n=HB)).then_inc(xt_loaded[r], 16)

            sp.wait_ge(S["ends_ready"], 1)
            for e in range(E):
                end = sp.value_load(tab[0:1, 2 * TILES + e:2 * TILES + e + 1], min_val=e * REGION,
                                    max_val=e * REGION + TOKENS)
                sp.dma_start(expert_rows[bass.ds(end, TR), :].rearrange("(p n) w -> p n w", n=HB), pad_rows[:, e])\
                    .then_inc(S["pads_stored"], 16)
            sp.wait_ge(S["table_ready"], 1)
            for i in range(2):
                sp.wait_ge(rows_scattered[i], 16 * NT * K * NB // 2)
            sp.wait_ge(S["pads_stored"], 16 * E)
            sp.wait_ge(S["spare_stored"], 16)
            for j in range(XR):
                load_tile(j, j)
            with sp.Fori(XR, LOOPED, XR) as j:
                for r in range(XR):
                    load_tile(j + r, r)
            for j in range(LOOPED, TILES):
                load_tile(j, j % XR)

            def load_y(n, r):
                need(sp, S["y_sum"], n - YR + 1)
                sp.dma_start(yb[r], y_v[:, bass.ds(n * TC, TC), :, :]).then_inc(yb_loaded[r], 16)

            for r in range(XR):
                sp.wait_ge(y_scattered[r], 16 * HB * len(range(r, TILES, XR)))
            for n in range(YR):
                load_y(n, n)
            with sp.Fori(YR, NB * NC - YR + 1, YR) as n:
                for r in range(YR):
                    load_y(n + r, r)
            for r in range(YR):
                sp.wait_ge(out_stored[r], 16 * NB * NC // YR)

        @block.gpsimd
        def _(pool):
            pool.memset(ident[:], 0.0).then_inc(S["pool_const"], 1)
            pool.memset(head_ones[:], 1.0).then_inc(S["pool_const"], 1)
            pool.memset(before[:], 1.0).then_inc(S["pool_const"], 1)
            pool.memset(ones_bf[:], 1.0).then_inc(S["pool_const"], 1)
            pool.memset(ones_col[:], 1.0).then_inc(S["pool_const"], 1)
            pool.memset(minus_half[:], -0.5).then_inc(S["pool_const"], 1)
            pool.memset(tile_start[:], 1.0).then_inc(S["pool_const"], 1)
            pool.memset(ones_e[:], 1.0).then_inc(S["pool_const"], 1)
            pool.wait_ge(S["pool_const"], 8)
            pool.affine_select(out=ident[:], in_=ident[:], compare_op=ALU.not_equal, fill=1.0, base=0,
                               pattern=[[-1, P]], channel_multiplier=1).then_inc(S["ident_ready"], 1)
            hv = head_ones[:].rearrange("p (g r) -> p g r", r=HD)
            pool.affine_select(out=hv, in_=hv, compare_op=ALU.is_ge, fill=0.0, base=0,
                               pattern=[[-HD, NH], [0, HD]], channel_multiplier=1).then_inc(S["ident_ready"], 1)
            pool.affine_select(out=before[:], in_=before[:], compare_op=ALU.is_gt, fill=0.0, base=0,
                               pattern=[[1, P]], channel_multiplier=-1).then_inc(S["ident_ready"], 1)
            tv = tile_start[:].rearrange("p (e t) -> p e t", e=E)
            pool.affine_select(out=tv, in_=tv, compare_op=ALU.not_equal, fill=0.0, base=0,
                               pattern=[[0, E], [1, NT]], channel_multiplier=0).then_inc(S["ident_ready"], 1)
            pool.wait_ge(S["ident_ready"], 4)
            pool.affine_select(out=hv, in_=hv, compare_op=ALU.is_ge, fill=0.0, base=HD - 1,
                               pattern=[[HD, NH], [0, HD]], channel_multiplier=-1).then_inc(S["ident_ready"], 1)
            iotas = [
                (iota_i[:, 0:E], [[1, E]], 0, 0),
                (iota_i[:, E:2 * E], [[REGION, E]], 0, 0),
                (iota_i[:, 2 * E:2 * E + NT * K], [[K * P, NT], [1, K]], 0, K),
                (iota_i[:, 32:32 + E * HB], [[P, E * HB]], YPAD0, 1),
                (iota_i[:, 64:64 + SPARE_TILES * HB], [[P, SPARE_TILES * HB]], YPAD0 + E * TR, 1),
                (iota_i[0:1, 96:96 + TILES], [[1, TILES]], 0, 0),
            ]
            for o, pattern, base, cm in iotas:
                pool.iota(o, pattern=pattern, base=base, channel_multiplier=cm).then_inc(S["iota_done"], 1)

            def power(out_, in_, ready, b, done):
                pool.wait_ge(ready, b + 1)
                pool.tensor_tensor(out_[:], in_[:], minus_half[:], ALU.pow).then_inc(done, 1)

            def norm(rstd, var, nmean, shift, ready, b, rstd_done, done):
                power(rstd, var, ready, b, rstd_done)
                pool.wait_ge(rstd_done, b + 1)
                pool.tensor_tensor(shift[:], nmean[:], rstd[:], ALU.mult).then_inc(done, 1)

            def norm1(b):
                norm(rstd1, var1, nmean1, shift1, S["var1_ready"], b, S["rstd1_ready"], S["norm1_ready"])

            def scatter(b, par, columns):
                for q in columns:
                    pool.indirect_dma_start(
                        expert_rows, bass.IndirectOffsetOnAxis(ap=slots[:, q:q + 1], axis=0),
                        rows[par][:, q % NT, q // NT, :], None).then_inc(rows_scattered[par], 16)

            def step(b, par, early, front, middle, back):
                if back:
                    wait_apart(pool, S["slots_ready"], b, S["pool_const"])
                    scatter(b - 1, 1 - par, range(0, 3 if front else 2))
                if middle:
                    norm(rstd2, var2, nmean2, shift2, S["var2_ready"], b, S["rstd2_ready"], S["norm2_ready"])
                if back:
                    scatter(b - 1, 1 - par, range(3 if front else 2, 7))
                if early:
                    norm1(b + 2)
                if back:
                    scatter(b - 1, 1 - par, range(7, 13))
                if front:
                    power(rstd3, var3, S["var3_ready"], b + 1, S["rstd3_ready"])
                if back:
                    scatter(b - 1, 1 - par, range(13, NT * K))

            norm1(0)
            pool.memset(pad_rows[:], 0.0).then_inc(S["pool_const"], 1)
            pool.memset(spare_rows, 0.0).then_inc(S["pool_const"], 1)
            for i in range(2):
                pool.memset(rows[i][:, :, :, D:W], 0.0).then_inc(S["pool_const"], 1)
            pipeline(pool, step)

            def put(j, r):
                wait_apart(pool, S["y_done"], j + 1, S["pool_const"])
                for i in range(HB):
                    pool.indirect_dma_start(
                        result_rows, bass.IndirectOffsetOnAxis(ap=meta[r][:, i, 0:1].bitcast(I32), axis=0),
                        ye[r][:, i, :], None).then_inc(y_scattered[r], 16)

            with pool.Fori(0, LOOPED, BODY) as j:
                for r in range(BODY):
                    put(j + r, r)
            for j in range(LOOPED, TILES):
                put(j, j % BODY)

        @block.tensor
        def _(pe):
            pe.wait_ge(S["ident_ready"], 5)
            pe.wait_ge(S["attn_w_loaded"], 16 * 5)
            pe.transpose(bank[0][:, 0:P], wraw[:, 0, :], ident[:])
            pe.transpose(bank[0][:, P:2 * P], wraw[:, 2, :], ident[:])
            pe.transpose(bank[0][:, 2 * P:3 * P], wraw[:, 3, :], ident[:])
            pe.transpose(bank[0][:, 3 * P:4 * P], wraw[:, 4, :], ident[:])
            pe.matmul(bank[1][:, 0:P], wraw[:, 1, :], head_ones[:], start=True, stop=True)\
                .then_inc(S["setup_psum"], 1)
            pe.wait_ge(S["mod_w_loaded"], 32)
            pe.wait_ge(S["csilu_ready"], 1)
            pe.transpose(bank[2][:, 0:NB], csilu[:], ident[0:NB, 0:NB]).then_inc(S["setup_psum"], 1)
            pe.wait_ge(S["setup_copied"], 2)
            half = 3 * D
            pe.matmul(bank[3][0:NB, 0:half], csiluT[:], wmod_sb[:, 0:half], start=True, stop=True)
            pe.matmul(bank[4][0:NB, 0:half], csiluT[:], wmod_sb[:, half:2 * half], start=True, stop=True)
            for i, m in enumerate((0, 1, 3, 4)):
                last = pe.matmul(bank[5][:, i * NB:(i + 1) * NB], wmod_sb[:, m * D:(m + 1) * D], csiluT[:],
                                 start=True, stop=True)
            last.then_inc(S["setup_psum"], 1)
            pe.wait_ge(S["ffn_w_loaded"], 16 * 5)
            for m in range(M):
                pe.transpose(bank[6][:, m * P:(m + 1) * P], sgraw[:, m, :], ident[:])
                pe.transpose(bank[6][:, (M + m) * P:(M + m + 1) * P], suraw[:, m, :], ident[:])
                pe.transpose(bank[7][:, m * P:(m + 1) * P], sdraw[:, m * P:(m + 1) * P], ident[:])
            pe.transpose(bank[7][:, M * P:M * P + E], rraw[:], ident[0:E, 0:E]).then_inc(S["setup_psum"], 1)
            pe.wait_ge(S["setup_copied"], 3)

            def step(b, par, early, front, middle, back):
                f, g, h = b + 1, b, b - 1

                def pair(q):
                    n, m = q // M, q % M
                    at = slice(n * CH, (n + 1) * CH)
                    for bank_, column, count, done in ((b_gate, m * P, "silu_ready", "gate_ready"),
                                                       (b_up, I + m * P, "gu_ready", "up_ready")):
                        if q > 0:
                            pe.wait_ge(S[count], 4 * h + q)
                        elif bank_ is b_gate:
                            pe.wait_ge(S["h2_lo_ready"], NC * (h + 1))
                        parts = ((Sgu_hi, h2_hi), (Sgu_hi, h2_lo), (Sgu_lo, h2_hi))
                        for i, (w, xs) in enumerate(parts):
                            last = pe.matmul(bank_[:], w[:, column:column + P], xs[:, at],
                                             start=(i == 0), stop=(i == len(parts) - 1))
                        last.then_inc(S[done], 1)

                def wo(n):
                    if n == 0:
                        pe.wait_ge(S["wo_scaled"], g + 1)
                    for t in range(TC):
                        at = (n * TC + t) * P
                        last = pe.matmul(b_O[n][:, t * P:(t + 1) * P], outT[:, at:at + P], Wo_b[:], start=True, stop=True)
                    last.then_inc(S["wo_ready"], 1)

                def turn_x(n):
                    if n == 0:
                        pe.wait_ge(S["xn1_ready"], NC * f + 1)
                    else:
                        pe.wait_ge(S["h1T_ready"], NC * f + n)
                    for t in range(TC):
                        last = pe.transpose(b_T[:, t * P:(t + 1) * P], xn1[:, n * TC + t, :], ident[:])
                    last.then_inc(S["xT_ready"], 1)

                def product(n, bank_, which):
                    at = slice(n * CH, (n + 1) * CH)
                    parts = ((Wa_hi, h1_hi[:]), (Wa_hi, h1_lo[:]), (Wa_lo, h1_hi[:])) if n == SPLIT_CHUNK \
                        else ((WaT, h1T[:, at]),)
                    for i, (w, xs) in enumerate(parts):
                        last = pe.matmul(bank_[:], w[:, which * P:(which + 1) * P], xs,
                                         start=(i == 0), stop=(i == len(parts) - 1))
                    return last

                def project(n):
                    if n > 0 and not middle:
                        pe.wait_ge(S["setup_copied"], 4)
                    if n == SPLIT_CHUNK:
                        pe.wait_ge(S["h1_lo_ready"], f + 1)
                    else:
                        pe.wait_ge(S["h1T_ready"], NC * f + n + 1)
                    product(n, b_proj[n][0], 0).then_inc(S["r_ready"], 1)
                    if n > 0 and back:
                        pe.wait_ge(S["gu_ready"], 4 * h + 4)
                    product(n, b_proj[n][1], 2).then_inc(S["w_ready"], 1)
                    pe.wait_ge(S["r_done"], NC * f + n + 1)
                    product(n, b_proj[n][0], 3).then_inc(S["ks_ready"], 1)
                    pe.wait_ge(S["w_done"], NC * f + n + 1)
                    product(n, b_proj[n][1], 1).then_inc(S["v_ready"], 1)

                def turn_x1(n):
                    if n == 0:
                        pe.wait_ge(S["xn2_done"], NC * g + 1)
                    else:
                        pe.wait_ge(S["h2T_ready"], NC * g + n)
                    for t in range(TC):
                        last = pe.transpose(b_T[:, t * P:(t + 1) * P], xn2[:, n * TC + t, :], ident[:])
                    last.then_inc(S["h2xT_ready"], 1)

                def turn_back(n):
                    pe.wait_ge(S["h2T_ready"], NC * g + n + 1)
                    for t in range(TC):
                        at = (n * TC + t) * P
                        last = pe.transpose(b_proj[0][n][:, t * P:(t + 1) * P], h2T[:, at:at + P], ident[:])
                    last.then_inc(S["h2_back"], 1)

                def down(n):
                    if n == 0:
                        pe.wait_ge(S["sd_scaled"], h + 1)
                    for t in range(TC):
                        at = (n * TC + t) * P
                        for m in range(M):
                            last = pe.matmul(b_O[n][:, t * P:(t + 1) * P], guT[:, m, at:at + P], Sd_b[:, m, :],
                                             start=(m == 0), stop=(m == M - 1))
                    last.then_inc(S["down_ready"], 1)

                def logits_of(n):
                    pe.wait_ge(S["h2T_ready"], NC * g + n + 1)
                    for t in range(n * TC, (n + 1) * TC):
                        last = pe.matmul(b_small[:, LG + t * E:LG + (t + 1) * E], h2T[:, t * P:(t + 1) * P],
                                         RwT[:], start=True, stop=True)
                    return last

                def squares(n):
                    pe.wait_ge(S["sq_ready"], NC * f + n + 1)
                    for t in range(n * TC, (n + 1) * TC):
                        last = pe.matmul(b_small[:, SS + t:SS + t + 1], sqT[:, t * P:(t + 1) * P], ones_col[:, 0:1],
                                         start=True, stop=True)
                    return last

                def ranks():
                    pe.wait_ge(S["picks_ready"], h + 1)
                    pe.matmul(b_small[:, PO:PO + E * NT], before[:], picks[:], start=True, stop=False)
                    pe.matmul(b_small[:, PO:PO + E * NT], ones_bf[:], picks_before[:], start=False, stop=True)
                    pe.matmul(b_small[:, CN:CN + E], ones_bf[:], picks_sum[:, NT - 1:E * NT:NT], start=True, stop=True)\
                        .then_inc(S["pos_ready"], 1)

                if back and not middle:
                    ranks()
                if middle and not front:
                    wo(0)
                    wo(1)
                    ranks()
                if back:
                    pair(0)
                if middle and front:
                    wo(0)
                    wo(1)
                if back:
                    pair(1)
                    if front:
                        ranks()
                if back:
                    pair(2)
                if front:
                    turn_x(0)
                if back:
                    pair(3)
                if front:
                    turn_x(1)
                    project(0)
                    project(1)
                if middle:
                    turn_x1(0)
                if back:
                    down(0)
                if front:
                    last = squares(0)
                if middle:
                    turn_x1(1)
                    logits_of(0)
                    turn_back(0)
                if back:
                    down(1)
                if middle:
                    turn_back(1)
                    last = logits_of(1)
                if front:
                    last = squares(1)
                if middle or front:
                    last.then_inc(S["small_ready"], 1)

            pipeline(pe, step)

            def turn(j, r):
                pe.wait_ge(xt_loaded[r], landed(j, r, XR))
                for i in range(HB):
                    if i == HB - 1:
                        need(pe, S["w_lo_done"], j)
                    last = pe.transpose(e_x[r % 2][:, i * P:(i + 1) * P], xt[r][:, i, 0:D], ident[:])
                last.then_inc(S["xtT_ready"], 1)

            def gate_up(j, r):
                pe.wait_ge(S["x_lo_done"], j + 1)
                for banks, at, done in ((e_gate, 0, "e_gate_ready"), (e_up, I, "e_up_ready")):
                    for m in range(M):
                        if at and m == M - 1:
                            need(pe, S["y_done"], j - 2)
                        block_ = slice(at + m * P, at + (m + 1) * P)
                        parts = ((w_hi, x_hi), (w_hi, x_lo), (w_lo, x_hi))
                        for i, (w, xs) in enumerate(parts):
                            last = pe.matmul(banks[r % 2][:, m * TR:(m + 1) * TR], w[r % 2][:, block_], xs[r % 2][:],
                                             start=(i == 0), stop=(i == len(parts) - 1))
                    last.then_inc(S[done], 1)

            def down(j, r, e):
                pe.wait_ge(S["gu_done"], j + 1)
                for i in range(HB):
                    for m in range(M):
                        last = pe.matmul(e_y[r % 2][:, i * D:(i + 1) * D], guTe[r % 2][:, m, i * P:(i + 1) * P],
                                         Wexp[:, bass.ds(e + (2 * I + m * D), D)], start=(m == 0), stop=(m == M - 1))
                last.then_inc(S["y_psum"], 1)

            def step_e(j, r, turns=True, gates=True):
                e = weights_of(j, mybir.EngineType.PE)
                if turns:
                    turn(j + 2, (r + 2) % BODY)
                elif gates:
                    pe.wait_ge(S["w_lo_done"], j + 2)
                if gates:
                    gate_up(j + 1, (r + 1) % BODY)
                down(j, r, e)

            pe.wait_ge(S["base_ready"], NB * NC)
            pe.wait_ge(S["h2T_ready"], NB * NC)
            pe.wait_ge(S["pos_done"], NB)
            pe.wait_ge(S["expert_w_loaded"], 16 * 3 * E)
            pe.wait_ge(S["table_ready"], 1)
            turn(0, 0)
            turn(1, 1)
            gate_up(0, 0)
            for j in range(BODY):
                step_e(j, j)
            with pe.Fori(BODY, LOOPED, BODY) as j:
                for q in range(BODY):
                    step_e(j + q, q)
            for j in range(LOOPED, TILES):
                step_e(j, j % BODY, turns=j + 2 < TILES, gates=j + 1 < TILES)

        @block.scalar
        def _(act):
            act.wait_ge(S["mod_w_loaded"], 32)
            act.activation(csilu[:], craw[:], ACT.Silu).then_inc(S["csilu_ready"], 1)

            def normalise(out_, src, shift, rstd, tiles):
                for t in tiles:
                    last = act.activation(out_[:, t, :], src(t), ACT.Identity, bias=shift[:, t:t + 1],
                                          scale=rstd[:, t:t + 1])
                return last

            def norm_x(b, par, n):
                if n == 0:
                    act.wait_ge(S["norm1_ready"], b + 1)
                normalise(xn1, lambda t: xb[par][:, t, :], shift1, rstd1, range(n * TC, (n + 1) * TC))\
                    .then_inc(S["xn1_ready"], 1)

            def touch(function):
                act.activation(touched[:], ones_e[0:1, 0:1], function).then_inc(S["touched"], 1)

            def step(b, par, early, front, middle, back):
                f, g = b + 1, b

                def split_h1():
                    act.wait_ge(S["h1T_ready"], NC * f + SPLIT_CHUNK + 1)
                    act.activation(h1_hi[:], h1T[:, SPLIT_CHUNK * CH:(SPLIT_CHUNK + 1) * CH], ACT.Copy)\
                        .then_inc(S["h1_hi_ready"], 1)

                def norm_x1(n):
                    act.wait_ge(S["norm2_ready"], g + 1)
                    normalise(xn2, lambda t: resid_tiles(g, t, 1), shift2, rstd2, range(n * TC, (n + 1) * TC))\
                        .then_inc(S["xn2_done"], 1)

                def rows_of(n):
                    at = slice(n * TC, (n + 1) * TC)
                    act.wait_ge(S["h2_back"], NC * g + n + 1)
                    act.activation(rows[par][:, at, :, 0:D],
                                   b_proj[0][n][:].rearrange("p (t d) -> p t d", d=D).unsqueeze(2)
                                   .to_broadcast([P, TC, K, D]), ACT.Copy).then_inc(S["rows_ready"], 1)

                def square(n):
                    at = slice(n * CH, (n + 1) * CH)
                    act.wait_ge(S["out_ready"], NC * f + n + 1)
                    act.activation(sqT[:, at], outT[:, at], ACT.Square).then_inc(S["sq_ready"], 1)

                def silu(q):
                    act.wait_ge(S["gate_ready"], 4 * (b - 1) + q + 1)
                    act.activation(sg[:, q, :], b_gate[:], ACT.Silu).then_inc(S["silu_ready"], 1)

                def modulate(n):
                    act.wait_ge(S["xT_ready"], NC * f + n + 1)
                    act.activation(h1T[:, n * CH:(n + 1) * CH], b_T[:], ACT.Identity, bias=cur_col[:, 0:1],
                                   scale=cur_col[:, 1:2]).then_inc(S["h1T_ready"], 1)

                if back:
                    silu(0)
                if front:
                    norm_x(f, 1 - par, 0)
                if back:
                    silu(1)
                if front:
                    norm_x(f, 1 - par, 1)
                if back:
                    silu(2)
                if front:
                    act.wait_ge(S["col_ready"], f + 1)
                    modulate(0)
                if back:
                    silu(3)
                if front:
                    touch(ACT.Sigmoid)
                    modulate(1)
                for n in range(NC):
                    at = slice(n * CH, (n + 1) * CH)
                    if front:
                        act.wait_ge(S["r_ready"], NC * f + n + 1)
                        act.activation(rT[:, at], b_proj[n][0][:], ACT.Sigmoid).then_inc(S["r_done"], 1)
                        if n == 0:
                            split_h1()
                        act.wait_ge(S["w_ready"], NC * f + n + 1)
                        act.activation(wsig[:, at], b_proj[n][1][:], ACT.Sigmoid).then_inc(S["w_done"], 1)
                        if n == NC - 1 and middle:
                            norm_x1(0)
                        act.wait_ge(S["ks_ready"], NC * f + n + 1)
                        act.activation(ksT[:, at], b_proj[n][0][:], ACT.Copy).then_inc(S["ks_done"], 1)
                        if n == NC - 1 and middle:
                            norm_x1(1)
                    elif middle:
                        norm_x1(n)
                if front:
                    square(0)
                if middle:
                    for n in range(NC):
                        block_ = slice(n * CH, (n + 1) * CH)
                        act.wait_ge(S["h2xT_ready"], NC * g + n + 1)
                        act.activation(h2T[:, block_], b_T[:], ACT.Identity, bias=cur_col2[:, 0:1], scale=cur_col2[:, 1:2])\
                            .then_inc(S["h2T_ready"], 1)
                        act.wait_ge(S["h2T_ready"], NC * g + n + 1)
                        act.activation(h2_hi[:, block_], h2T[:, block_], ACT.Copy).then_inc(S["h2_hi_ready"], 1)
                if front:
                    square(1)
                if middle:
                    for n in range(NC):
                        rows_of(n)
                if middle:
                    act.wait_ge(S["logits_ready"], g + 1)
                    act.activation(probs[:], logits[:], ACT.Sigmoid).then_inc(S["probs_ready"], 1)
                    touch(ACT.Silu)

            pipeline(act, step)

            def split_x(j, r):
                act.wait_ge(S["xtT_ready"], j + 1)
                act.activation(x_hi[r % 2][:], e_x[r % 2][:, 0:TR], ACT.Copy).then_inc(S["x_hi_done"], 1)

            def split_w(j, r, e):
                act.activation(w_hi[r % 2], Wexp[:, bass.ds(e, 2 * I)], ACT.Copy).then_inc(S["w_hi_done"], 1)

            def silu(j, r):
                act.wait_ge(S["e_gate_ready"], j + 1)
                act.activation(sge[r % 2], e_gate[r % 2][:], ACT.Silu).then_inc(S["silu_done"], 1)

            def scale_y(j, r):
                act.wait_ge(S["y_psum"], j + 1)
                act.wait_ge(S["meta_done"], j + 1)
                for i in range(HB):
                    last = act.activation(ye[r][:, i, :], e_y[r % 2][:, i * D:(i + 1) * D], ACT.Copy,
                                          scale=meta[r][:, i, 1:2])
                last.then_inc(S["y_done"], 1)

            def step_e(j, r, turns=True, scales=True):
                if turns:
                    e = weights_of(j + 2, mybir.EngineType.Activation)
                silu(j, r)
                if turns:
                    split_x(j + 2, (r + 2) % BODY)
                    split_w(j + 2, (r + 2) % BODY, e)
                if scales:
                    scale_y(j - 1, (r - 1) % BODY)

            act.wait_ge(S["expert_w_loaded"], 16 * 3 * E)
            act.wait_ge(S["table_ready"], 1)
            for j in range(2):
                split_x(j, j)
                split_w(j, j, weights_of(j, mybir.EngineType.Activation))
            for j in range(BODY):
                step_e(j, j, scales=j > 0)
            with act.Fori(BODY, LOOPED, BODY) as j:
                for q in range(BODY):
                    step_e(j + q, q)
            for j in range(LOOPED, TILES):
                step_e(j, j % BODY, turns=j + 2 < TILES)
            scale_y(TILES - 1, (TILES - 1) % BODY)

            with act.Fori(0, NB * NC - YR + 1, YR) as n:
                for r in range(YR):
                    act.wait_ge(S["fin_ready"], n + r + 1)
                    act.dma_start(out_v[:, bass.ds((n + r) * TC, TC), :], fin[r]).then_inc(out_stored[r], 16)

        @block.vector
        def _(dve):
            def stats_of(src, stats, s_stats):
                for t in range(NT):
                    last = dve.bn_stats(stats[:, t, :], src(t))
                last.then_inc(s_stats, 1)

            def norm_of(stats, mv, var, nmean, count, s_stats, s_mv, s_var, free=None, between=None):
                wait_apart(dve, s_stats, count, S["dve_const"])
                for t in range(NT):
                    last = dve.bn_aggr(mv[:, t, :], stats[:, t, :])
                last.then_inc(s_mv, 1)
                if between:
                    between()
                if free:
                    free()
                dve.wait_ge(s_mv, count)
                dve.tensor_scalar(var[:], mv[:, :, 1], LN_EPS, None, ALU.add)
                dve.tensor_scalar(nmean[:], mv[:, :, 0], -1.0, None, ALU.mult).then_inc(s_var, 1)

            def stats_x(b, par):
                wait_apart(dve, x_loaded[par], landed(b, par, 2), S["dve_const"])
                stats_of(lambda t: xb[par][:, t, :], stats1, S["stats1_done"])

            def norm_x(b, between=None):
                norm_of(stats1, mv1, var1, nmean1, b + 1, S["stats1_done"], S["mv1_done"], S["var1_ready"],
                        lambda: need(dve, S["xn1_ready"], NC * b), between)

            def columns(b):
                dve.tensor_copy(cur_col[:], mod_col[:, bass.ds(b * COLS, 2)]).then_inc(S["col_ready"], 1)

            stats_x(0, 0)
            norm_x(0)
            dve.wait_ge(S["iota_done"], 6)
            dve.tensor_copy(expert_iota[:], iota_i[:, 0:E])
            dve.tensor_copy(region_rows[:], iota_i[:, E:2 * E])
            dve.tensor_copy(running[:], iota_i[:, E:2 * E])
            dve.tensor_copy(dest_next[:], iota_i[:, 2 * E:2 * E + NT * K].rearrange("p (t k) -> p t k", k=K))
            dve.tensor_copy(tile_iota[:], iota_i[0:1, 96:96 + TILES]).then_inc(S["dve_const"], 1)
            dve.wait_ge(S["dve_const"], 1)
            dve.wait_ge(S["setup_psum"], 1)
            dve.tensor_copy(WoT[:], bank[0][:, 3 * P:4 * P])
            dve.tensor_copy(WaT[:, 0:3 * P], bank[0][:, 0:3 * P])
            dve.tensor_copy(WaT[:, 3 * P:4 * P], bank[1][:, 0:P])
            dve.tensor_copy(Wa_hi[:, 0:3 * P], bank[0][:, 0:3 * P])
            dve.tensor_copy(Wa_hi[:, 3 * P:4 * P], bank[1][:, 0:P]).then_inc(S["split_step"], 1)
            dve.wait_ge(S["split_step"], 1)
            dve.tensor_tensor(Wa_lo[:, 0:3 * P], bank[0][:, 0:3 * P], Wa_hi[:, 0:3 * P].bitcast(F32), ALU.subtract)
            dve.tensor_tensor(Wa_lo[:, 3 * P:4 * P], bank[1][:, 0:P], Wa_hi[:, 3 * P:4 * P].bitcast(F32), ALU.subtract)\
                .then_inc(S["setup_copied"], 1)
            dve.wait_ge(S["setup_psum"], 2)
            dve.tensor_copy(csiluT[:], bank[2][:, 0:NB]).then_inc(S["setup_copied"], 1)
            dve.wait_ge(S["setup_psum"], 3)
            mod_f = mod_sb[:].rearrange("b m d -> b (m d)")
            dve.tensor_copy(mod_f[:, 0:3 * D], bank[3][0:NB, 0:3 * D])
            dve.tensor_copy(mod_f[:, 3 * D:6 * D], bank[4][0:NB, 0:3 * D])
            for i in range(COLS):
                last = dve.tensor_scalar(mod_col[:, i:COLS * NB:COLS], bank[5][:, i * NB:(i + 1) * NB], float(i % 2), None,
                                         ALU.add)
            last.then_inc(S["setup_copied"], 1)
            dve.wait_ge(S["setup_copied"], 3)
            columns(0)
            gates = mod_sb[:, 2:6:3, :]
            dve.tensor_scalar(sign_sb[:], gates, 0.0, 2.0, ALU.is_ge, ALU.mult)
            dve.scalar_tensor_tensor(out=mag_sb[:], in0=gates, scalar=-1.0, in1=gates, op0=ALU.mult, op1=ALU.max)\
                .then_inc(S["mod_step"], 1)
            dve.wait_ge(S["mod_step"], 1)
            dve.tensor_scalar(mag_sb[:], mag_sb[:], 0.25, None, ALU.max).then_inc(S["mod_step"], 1)
            dve.wait_ge(S["mod_step"], 2)
            dve.scalar_tensor_tensor(out=gates, in0=sign_sb[:], scalar=-1.0, in1=mag_sb[:], op0=ALU.add, op1=ALU.mult)\
                .then_inc(S["mod_ready"], 1)
            dve.wait_ge(S["setup_psum"], 4)
            dve.tensor_copy(Sgu_hi[:], bank[6][:, 0:2 * I]).then_inc(S["mod_step"], 1)
            dve.wait_ge(S["mod_step"], 3)
            dve.tensor_tensor(Sgu_lo[:], bank[6][:, 0:2 * I], Sgu_hi[:].bitcast(F32), ALU.subtract)
            dve.tensor_copy(SdT[:].rearrange("p m h -> p (m h)"), bank[7][:, 0:M * P])
            dve.tensor_copy(RwT[:], bank[7][:, M * P:M * P + E]).then_inc(S["setup_copied"], 1)
            dve.wait_ge(S["setup_copied"], 4)

            def scattered(b, par):
                batch = 16 * K * NT
                return (batch // 2) * b - (batch // 2) * par

            def make_table():
                count = [0]

                def then(instruction):
                    count[0] += 1
                    instruction.then_inc(S["table_step"], 1)
                    dve.wait_ge(S["table_step"], count[0])

                dve.tensor_copy(tab[:, 2 * TILES:2 * TILES + E], tmpf[0:1, :]).then_inc(S["ends_ready"], 1)
                then(dve.tensor_tensor(counts[:], tmpf[:], region_rows[:], ALU.subtract))
                then(dve.tensor_scalar(tmpi[:], counts[:], float(TR - 1), None, ALU.add))
                then(dve.tensor_scalar(tilesi[:], tmpi[:], TR.bit_length() - 1, None, ALU.arith_shift_right))
                then(dve.tensor_copy(tilesf[:], tilesi[:]))
                then(dve.tensor_tensor_scan(ends[:], ones_e[:], tilesf[:], 0.0, ALU.mult, ALU.add))
                then(dve.tensor_scalar(skip[:], tilesf[:], -1.0, float(REGION // TR), ALU.mult, ALU.add))
                over_e = lambda a: a.unsqueeze(1).to_broadcast([1, TILES, E])
                then(dve.tensor_tensor(passed[:], tile_iota[:].unsqueeze(2).to_broadcast([1, TILES, E]),
                                       over_e(ends[0:1, :]), ALU.is_ge))
                then(dve.tensor_tensor(passed_skip[:], passed[:], over_e(skip[0:1, :]), ALU.mult))
                dve.tensor_reduce(tab_f[:, 0, :], passed[:], AX_X, ALU.add)
                then(dve.tensor_reduce(tab_f[:, 1, :], passed_skip[:], AX_X, ALU.add))
                then(dve.tensor_tensor(tab_g[:, 1, :], tab_f[:, 1, :], tile_iota[:], ALU.add))
                dve.tensor_scalar(tab[:, TILES:2 * TILES], tab_g[:, 1, :], float(TR), None, ALU.mult)
                dve.tensor_scalar(tab[:, 0:TILES], tab_f[:, 0, :], float(E - 1), float(WE), ALU.min, ALU.mult).then_inc(S["table_ready"], 1)

            def step(b, par, early, front, middle, back):
                f, g, h = b + 1, b, b - 1

                def mult(q):
                    n, m = q // M, q % M
                    dve.wait_ge(S["up_ready"], 4 * h + q + 1)
                    dve.wait_ge(S["silu_ready"], 4 * h + q + 1)
                    if q == 0:
                        need(dve, S["down_ready"], NC * h)
                    dve.tensor_tensor(guT[:, m, n * CH:(n + 1) * CH], sg[:, q, :], b_up[:], ALU.mult)\
                        .then_inc(S["gu_ready"], 1)

                def add_x(n, tiles=range(TC)):
                    if not tiles:
                        return
                    if n == 0 and tiles[0] == 0:
                        if isinstance(g, int) and g == 0:
                            dve.wait_ge(S["spare_stored"], 16)
                        dve.wait_ge(S["rstd3_ready"], g + 1)
                    if tiles[0] == 0:
                        dve.wait_ge(S["wo_ready"], NC * g + n + 1)
                    for t in (n * TC + i for i in tiles):
                        last = dve.scalar_tensor_tensor(
                            out=resid_tiles(g, t, 1), in0=b_O[n][:, (t % TC) * P:(t % TC + 1) * P],
                            scalar=rstd3[:, t:t + 1], in1=xb[par][:, t, :], op0=ALU.mult, op1=ALU.add)
                    if n == NC - 1 and tiles[-1] == TC - 1:
                        last.then_inc(S["x1_ready"], 1)

                def split_h1():
                    dve.wait_ge(S["h1_hi_ready"], f + 1)
                    dve.tensor_tensor(h1_lo[:], h1T[:, SPLIT_CHUNK * CH:(SPLIT_CHUNK + 1) * CH], h1_hi[:].bitcast(F32),
                                      ALU.subtract).then_inc(S["h1_lo_ready"], 1)

                def decay(n):
                    at = slice(n * CH, (n + 1) * CH)
                    dve.wait_ge(S["w_done"], NC * f + n + 1)
                    dve.tensor_scalar(wsig[:, at], wsig[:, at], 0.99, None, ALU.mult)

                def times_v(n):
                    at = slice(n * CH, (n + 1) * CH)
                    dve.wait_ge(S["ks_done"], NC * f + n + 1)
                    dve.wait_ge(S["v_ready"], NC * f + n + 1)
                    dve.tensor_tensor(ksT[:, at], ksT[:, at], b_proj[n][1][:], ALU.mult).then_inc(S["kv_done"], 1)

                def scan(n):
                    at = slice(n * CH, (n + 1) * CH)
                    dve.wait_ge(S["kv_done"], NC * f + n + 1)
                    dve.tensor_tensor_scan(stateT[:, at], wsig[:, at], ksT[:, at],
                                           0.0 if n == 0 else stateT[:, n * CH - 1:n * CH], ALU.mult, ALU.add)\
                        .then_inc(S["state_done"], 1)

                def read_state(n):
                    at = slice(n * CH, (n + 1) * CH)
                    dve.wait_ge(S["state_done"], NC * f + n + 1)
                    dve.tensor_tensor(outT[:, at], stateT[:, at], rT[:, at], ALU.mult).then_inc(S["out_ready"], 1)

                def pick():
                    dve.wait_ge(S["onehot_done"], h + 1)
                    dve.tensor_tensor(picks[:].rearrange("p (e t) -> p t e", e=E), onehot[:, 0], onehot[:, 1], ALU.add)\
                        .then_inc(S["picks_done"], 1)
                    dve.wait_ge(S["picks_done"], h + 1)
                    dve.tensor_tensor_scan(picks_sum[:], tile_start[:], picks[:], 0.0, ALU.mult, ALU.add)\
                        .then_inc(S["picks_sum_done"], 1)
                    dve.wait_ge(S["picks_sum_done"], h + 1)
                    dve.tensor_tensor(picks_before[:], picks_sum[:], picks[:], ALU.subtract).then_inc(S["picks_ready"], 1)
                    dve.wait_ge(S["rden_done"], h + 1)
                    dve.tensor_tensor(rows[1 - par][:, :, :, D + 1], top[:, :, 0:K],
                                      rden[:].unsqueeze(2).to_broadcast([P, NT, K]), ALU.mult)
                    dve.tensor_copy(rows[1 - par][:, :, :, D].bitcast(I32), dest_next[:]).then_inc(S["meta_ready"], 1)
                    dve.wait_ge(S["meta_ready"], h + 1)
                    dve.tensor_scalar(dest_next[:], dest_next[:], float(K * T), None, ALU.add)

                def find_slots(adds=False):
                    between = lambda t: add_x(1, range(t, t + 1) if adds else ())
                    dve.wait_ge(S["pos_ready"], h + 1)
                    ev = lambda a: a.rearrange("p (e t) -> p e t", e=E)
                    dve.tensor_tensor(ev(pos[:]), ev(b_small[:, PO:PO + E * NT]),
                                      running[:].unsqueeze(2).to_broadcast([P, E, NT]), ALU.add)
                    dve.tensor_tensor(tmpf[:], running[:], b_small[:, CN:CN + E], ALU.add).then_inc(S["pos_done"], 1)
                    between(0)
                    dve.wait_ge(S["pos_done"], h + 1)
                    dve.tensor_copy(running[:], tmpf[:])
                    pv = pos[:].rearrange("p (e t) -> p t e", e=E)
                    for k in range(K):
                        last = dve.tensor_tensor(prod[:, k], onehot[:, k], pv, ALU.mult)
                    last.then_inc(S["prod_done"], 1)
                    if adds:
                        mult(2)
                    between(1)
                    dve.wait_ge(S["prod_done"], h + 1)
                    dve.tensor_reduce(slotf[:], prod[:].rearrange("p k t e -> p (k t) e"), AX_X, ALU.add)\
                        .then_inc(S["slotf_done"], 1)
                    between(2)
                    dve.wait_ge(S["slotf_done"], h + 1)
                    need(dve, rows_scattered[par], scattered(b, par))
                    dve.tensor_copy(slots[:], slotf[:]).then_inc(S["slots_ready"], 1)
                    between(3)

                def norm_x1(between=None):
                    dve.tensor_copy(cur_col2[:], mod_col[:, bass.ds(g * COLS + 2, 2)])
                    wait_apart(dve, S["x1_ready"], g + 1, S["dve_const"])
                    stats_of(lambda t: resid_tiles(g, t, 1), stats2, S["stats2_done"])
                    norm_of(stats2, mv2, var2, nmean2, g + 1, S["stats2_done"], S["mv2_done"], S["var2_ready"],
                            between=between)

                if not middle and back:
                    pick()
                    find_slots()
                    make_table()
                if middle and not front:
                    pick()
                    add_x(0)
                    add_x(1)
                    find_slots()
                    norm_x1()
                if back:
                    mult(0)
                    if front:
                        pick()
                if middle and front and not back:
                    add_x(0)
                if back:
                    mult(1)
                    if front:
                        add_x(0)
                    if front:
                        find_slots(adds=True)
                elif middle:
                    add_x(1)
                if back and not front:
                    mult(2)
                if middle and front:
                    norm_x1(between=split_h1)
                if back:
                    mult(3)
                    dve.wait_ge(S["mod_row_loaded"], 16)
                    need(dve, S["down_ready"], NC * h)
                    for m in range(M):
                        last = dve.tensor_tensor(Sd_b[:, m, :], SdT[:, m, :], mod_at(h, 1), ALU.mult)
                    last.then_inc(S["sd_scaled"], 1)
                if early:
                    stats_x(b + 2, par)
                if front and not middle:
                    split_h1()
                if front:
                    decay(0)
                    times_v(0)
                if early:
                    norm_x(b + 2, lambda: scan(0))
                elif front:
                    scan(0)
                def split_h2(n):
                    at = slice(n * CH, (n + 1) * CH)
                    dve.wait_ge(S["h2_hi_ready"], NC * g + n + 1)
                    dve.tensor_tensor(h2_lo[:, at], h2T[:, at], h2_hi[:, at].bitcast(F32), ALU.subtract)\
                        .then_inc(S["h2_lo_ready"], 1)

                def add_base(n):
                    dve.wait_ge(S["down_ready"], NC * h + n + 1)
                    tiles = resid_tiles(h, n * TC, TC)
                    dve.tensor_tensor(tiles, b_O[n][:], tiles, ALU.add).then_inc(S["base_ready"], 1)

                if front:
                    read_state(0)
                    decay(1)
                    times_v(1)
                    scan(1)
                    read_state(1)
                if back:
                    add_base(0)
                if middle:
                    split_h2(0)
                if early:
                    columns(b + 2)
                if back:
                    add_base(1)
                if middle:
                    split_h2(1)
                if front or middle:
                    dve.wait_ge(S["small_ready"], b + 2)
                if middle:
                    dve.tensor_tensor(logits[:], b_small[:, LG:LG + NT * E].rearrange("p (t e) -> p t e", e=E),
                                      bias_row[:].unsqueeze(1).to_broadcast([P, NT, E]), ALU.add)\
                        .then_inc(S["logits_ready"], 1)
                if front:
                    dve.tensor_scalar(var3[:], b_small[:, SS:SS + NT], 1.0 / D, RMS_EPS, ALU.mult, ALU.add)\
                        .then_inc(S["var3_ready"], 1)
                if front:
                    dve.wait_ge(S["mod_row_loaded"], 16)
                    dve.tensor_tensor(Wo_b[:], WoT[:], mod_at(f, 0), ALU.mult).then_inc(S["wo_scaled"], 1)
                if middle:
                    wait_apart(dve, S["probs_ready"], g + 1, S["dve_const"])
                    for t in range(NT):
                        last = dve.max(top[:, t, :], probs[:, t, :])
                    last.then_inc(S["top_done"], 1)
                    wait_apart(dve, S["top_done"], g + 1, S["dve_const"])
                    for t in range(NT):
                        last = dve.max_index(topi[:, t, :], top[:, t, :], probs[:, t, :])
                    last.then_inc(S["topi_done"], 1)
                    dve.tensor_tensor(den[:], top[:, :, 0], top[:, :, 1], ALU.add).then_inc(S["den_done"], 1)
                    dve.wait_ge(S["topi_done"], g + 1)
                    dve.tensor_copy(topf[:], topi[:, :, 0:K].rearrange("p t k -> p k t")).then_inc(S["topf_done"], 1)
                    dve.wait_ge(S["den_done"], g + 1)
                    dve.reciprocal(rden[:], den[:]).then_inc(S["rden_done"], 1)
                    dve.wait_ge(S["topf_done"], g + 1)
                    for k in range(K):
                        last = dve.tensor_tensor(onehot[:, k], topf[:, k, :].unsqueeze(2).to_broadcast([P, NT, E]),
                                                 expert_iota[:].unsqueeze(1).to_broadcast([P, NT, E]), ALU.is_equal)
                    last.then_inc(S["onehot_done"], 1)

            dve.wait_ge(S["pool_const"], 12)
            dve.tensor_copy(spare_rows[:, :, D:D + 1].bitcast(I32).rearrange("p t o -> p (t o)"),
                            iota_i[:, 64:64 + SPARE_TILES * HB]).then_inc(S["spare_ready"], 1)
            dve.tensor_copy(pad_rows[:].rearrange("p e n w -> p (e n) w")[:, :, D:D + 1].bitcast(I32).rearrange("p t o -> p (t o)"),
                            iota_i[:, 32:32 + E * HB])
            pipeline(dve, step)

            def mult_e(j, r):
                dve.wait_ge(S["e_up_ready"], j + 1)
                dve.wait_ge(S["silu_done"], j + 1)
                dve.tensor_tensor(guTe[r % 2].rearrange("p m t -> p (m t)"), sge[r % 2], e_up[r % 2][:], ALU.mult)\
                    .then_inc(S["gu_done"], 1)

            def split_x(j, r):
                dve.wait_ge(S["x_hi_done"], j + 1)
                dve.tensor_tensor(x_lo[r % 2][:], e_x[r % 2][:, 0:TR], x_hi[r % 2][:].bitcast(F32), ALU.subtract)\
                    .then_inc(S["x_lo_done"], 1)

            def split_w(j, r, e):
                dve.wait_ge(S["w_hi_done"], j + 1)
                dve.tensor_tensor(w_lo[r % 2], Wexp[:, bass.ds(e, 2 * I)], w_hi[r % 2].bitcast(F32), ALU.subtract)\
                    .then_inc(S["w_lo_done"], 1)

            def copy_meta(j, r):
                dve.wait_ge(xt_loaded[r], landed(j, r, XR))
                need(dve, y_scattered[r], (16 * HB // XR) * j - (16 * HB // XR) * r)
                dve.tensor_copy(meta[r][:], xt[r][:, :, D:D + 2]).then_inc(S["meta_done"], 1)

            def step_e(j, r, splits=True):
                if splits:
                    e = weights_of(j + 2, mybir.EngineType.DVE)
                mult_e(j, r)
                if splits:
                    split_x(j + 2, (r + 2) % BODY)
                    split_w(j + 2, (r + 2) % BODY, e)
                copy_meta(j, r)

            dve.wait_ge(S["expert_w_loaded"], 16 * 3 * E)
            dve.wait_ge(S["table_ready"], 1)
            for j in range(2):
                split_x(j, j)
                split_w(j, j, weights_of(j, mybir.EngineType.DVE))
            for j in range(BODY):
                step_e(j, j)
            with dve.Fori(BODY, LOOPED, BODY) as j:
                for q in range(BODY):
                    step_e(j + q, q)
            for j in range(LOOPED, TILES):
                step_e(j, j % BODY, splits=j + 2 < TILES)

            def combine(b, half):
                over = lambda a: a.unsqueeze(1).to_broadcast([P, TC, D])
                for n in range(NC):
                    dve.wait_ge(yb_loaded[half * NC + n], landed(b, half, 2, 16))
                    y = yb[half * NC + n]
                    dve.tensor_tensor(acc[half * NC + n], y[:, :, 0, :], y[:, :, 1, :], ALU.add).then_inc(S["y_sum"], 1)
                for n in range(NC):
                    dve.wait_ge(S["y_sum"], NC * b + n + 1)
                    dve.tensor_tensor(acc[half * NC + n], acc[half * NC + n], over(mod_at(b, 1)), ALU.mult).then_inc(S["y_gated"], 1)
                for n in range(NC):
                    dve.wait_ge(S["y_gated"], NC * b + n + 1)
                    need(dve, out_stored[half * NC + n], 8 * b - 8 * half)
                    dve.tensor_tensor(fin[half * NC + n].rearrange("p t d -> p (t d)"),
                                      acc[half * NC + n].rearrange("p t d -> p (t d)"),
                                      resid_tiles(b, n * TC, TC), ALU.add).then_inc(S["fin_ready"], 1)

            combine(0, 0)
            combine(1, 1)
            with dve.Fori(2, NB - 1, 2) as b:
                combine(b, 0)
                combine(b + 1, 1)


_INS = ["L0_attn_x", "L0_attn_Wr", "L0_attn_Wk", "L0_attn_Wv", "L0_attn_Ww", "L0_attn_Wo", "L0_ffn_shared_gate",
        "L0_ffn_shared_up", "L0_ffn_shared_down", "L0_ffn_gate_w", "L0_ffn_up_w", "L0_ffn_down_w",
        "L0_ffn_router_w", "L0_ffn_routing_bias", "L0_c", "L0_wmod"]


def kernel(**inputs):
    import numpy as np
    import concourse.bacc as bacc
    from concourse.bass_utils import run_bass_kernel_spmd

    nc = bacc.Bacc("TRN2", target_bir_lowering=False, num_devices=1)
    arrays, args = {}, []
    for name in _INS:
        a = np.ascontiguousarray(inputs[name])
        arrays[f"in_{name}"] = a
        args.append(nc.dram_tensor(f"in_{name}", a.shape, mybir.dt.from_np(a.dtype), kind="ExternalInput").ap())
    out = nc.dram_tensor("out_0", inputs["L0_attn_x"].shape, F32, kind="ExternalOutput").ap()
    build(nc, *args, out)
    r = run_bass_kernel_spmd(nc, [arrays], core_ids=[0])
    return r.results[0]["out_0"]
```
